# Optimizing a Trainium2 kernel written in Bass

```python
import numpy as np
import jax
import jax.numpy as jnp

def _softmax(x, axis=-1):
    return jax.nn.softmax(x, axis=axis)

def _gelu(x):
    return jax.nn.gelu(x, approximate=True)

def _silu(x):
    return jax.nn.silu(x)

def _sigmoid(x):
    return jax.nn.sigmoid(x)

def _layernorm(x, axis=-1, eps=1e-05):
    m = jnp.mean(x, axis=axis, keepdims=True)
    v = jnp.var(x, axis=axis, keepdims=True)
    return (x - m) / jnp.sqrt(v + eps)

def _scatter_add(tgt, idx, src, axis=0):
    return tgt.at[idx].add(src)

def _segment_sum(src, seg, n):
    return jax.ops.segment_sum(src, seg, n)
kernel_name = 'mk_seq_postln_d1_jaxref_r8_1320ba'

def setup_inputs(seed: int=0):
    np.random.seed(seed)
    _w = jnp.asarray

    def _L0_attn_setup():
        import jax, jax.numpy as jnp
        import numpy as np
        EPS_NORM = 1e-05
        EPS_L2 = 1e-06
        CHUNK = 128

        def _short_conv(x, w):
            K = w.shape[1]
            T = x.shape[1]
            xp = jnp.pad(x, ((0, 0), (K - 1, 0), (0, 0)))
            y = sum((xp[:, i:i + T, :] * w[:, i] for i in range(K)))
            return jax.nn.silu(y)

        def _l2norm(x):
            return x * jax.lax.rsqrt(jnp.sum(x * x, axis=-1, keepdims=True) + EPS_L2)

        def _kda_scan(q, k, v, gk, beta):
            B, T, H, Dk = q.shape
            Dv = v.shape[-1]
            NC = T // CHUNK

            def c4(x):
                return jnp.transpose(x.reshape(B, NC, CHUNK, H, x.shape[-1]), (1, 2, 0, 3, 4))
            qc, kc, vc, gc = (c4(q), c4(k), c4(v), c4(gk))
            bc = jnp.transpose(beta.reshape(B, NC, CHUNK, H), (1, 2, 0, 3))

            def step(S, inp):
                q_t, k_t, v_t, g_t, b_t = inp
                S = S * jnp.exp(g_t)[..., None]
                err = v_t - jnp.einsum('bhk,bhkv->bhv', k_t, S)
                S = S + b_t[..., None, None] * (k_t[..., None] * err[..., None, :])
                o_t = jnp.einsum('bhk,bhkv->bhv', q_t, S)
                return (S, o_t)

            @jax.checkpoint
            def chunk_fn(S, xs):
                return jax.lax.scan(step, S, xs)
            S0 = jnp.zeros((B, H, Dk, Dv), q.dtype)
            _, o = jax.lax.scan(chunk_fn, S0, (qc, kc, vc, gc, bc))
            return jnp.transpose(o.reshape(T, B, H, Dv), (1, 0, 2, 3))

        def _forward(hidden_states, q_w, k_w, v_w, q_conv_w, k_conv_w, v_conv_w, f_w1, f_w2, b_w, A_log, dt_bias, g_w1, g_w2, g_b2, o_norm_w, o_w):
            B, T, D = hidden_states.shape
            H = A_log.shape[0]
            Dv = o_norm_w.shape[0]
            Dk = q_w.shape[1] // H
            q = _short_conv(hidden_states @ q_w, q_conv_w).reshape(B, T, H, Dk)
            k = _short_conv(hidden_states @ k_w, k_conv_w).reshape(B, T, H, Dk)
            v = _short_conv(hidden_states @ v_w, v_conv_w).reshape(B, T, H, Dv)
            g = (hidden_states @ f_w1 @ f_w2).reshape(B, T, H, Dk)
            gk = -jnp.exp(A_log)[:, None] * jax.nn.softplus(g + dt_bias.reshape(H, Dk))
            beta = jax.nn.sigmoid(hidden_states @ b_w)
            q = _l2norm(q) * Dk ** (-0.5)
            k = _l2norm(k)
            o = _kda_scan(q, k, v, gk, beta)
            gate = (hidden_states @ g_w1 @ g_w2 + g_b2).reshape(B, T, H, Dv)
            o = o * jax.lax.rsqrt(jnp.mean(o * o, axis=-1, keepdims=True) + EPS_NORM) * o_norm_w
            o = o * jax.nn.sigmoid(gate)
            return o.reshape(B, T, H * Dv) @ o_w
        key = jax.random.key(seed)
        B, T, D = (2, 512, 256)
        H, Dk, Dv = (16, 128, 128)
        KD, VD = (H * Dk, H * Dv)
        Kc = 4
        ks = jax.random.split(key, 16)
        s = 0.02
        n = lambda kk, sh: jax.random.normal(kk, sh, jnp.float32) * s
        return dict(hidden_states=jax.random.normal(ks[0], (B, T, D), jnp.float32), q_w=n(ks[1], (D, KD)), k_w=n(ks[2], (D, KD)), v_w=n(ks[3], (D, VD)), q_conv_w=n(ks[4], (KD, Kc)), k_conv_w=n(ks[5], (KD, Kc)), v_conv_w=n(ks[6], (VD, Kc)), f_w1=n(ks[7], (D, Dv)), f_w2=n(ks[8], (Dv, KD)), b_w=n(ks[9], (D, H)), A_log=jnp.log(jax.random.uniform(ks[10], (H,), jnp.float32, 1.0, 16.0)), dt_bias=jnp.zeros((KD,), jnp.float32), g_w1=n(ks[11], (D, Dv)), g_w2=n(ks[12], (Dv, VD)), g_b2=jnp.zeros((VD,), jnp.float32), o_norm_w=jnp.ones((Dv,), jnp.float32), o_w=n(ks[13], (VD, D)))
    _L0_attn_in = _L0_attn_setup()

    def _L0_ffn_setup():
        import jax, jax.numpy as jnp
        import numpy as np
        TOPK = 2
        NORM_TOPK = True
        SCALE = 1.0
        EPS = 1e-09
        key = jax.random.key(seed)
        ks = jax.random.split(key, 9)
        h, i, E = (256, 128, 16)
        std = 0.02
        return {'x': jax.random.normal(ks[0], (1, 256, h), jnp.float32), 'Wr': jax.random.normal(ks[1], (E, h), jnp.float32) * std, 'bias': jnp.zeros((E,), jnp.float32), 'Wg': jax.random.normal(ks[2], (E, h, i), jnp.float32) * std, 'Wu': jax.random.normal(ks[3], (E, h, i), jnp.float32) * std, 'Wd': jax.random.normal(ks[4], (E, i, h), jnp.float32) * std, 'sWg': jax.random.normal(ks[5], (h, i), jnp.float32) * std, 'sWu': jax.random.normal(ks[6], (h, i), jnp.float32) * std, 'sWd': jax.random.normal(ks[7], (i, h), jnp.float32) * std}
    _L0_ffn_in = _L0_ffn_setup()
    _d = {'L0_attn_hidden_states': _L0_attn_in['hidden_states'], 'L0_attn_q_w': _L0_attn_in['q_w'], 'L0_attn_k_w': _L0_attn_in['k_w'], 'L0_attn_v_w': _L0_attn_in['v_w'], 'L0_attn_q_conv_w': _L0_attn_in['q_conv_w'], 'L0_attn_k_conv_w': _L0_attn_in['k_conv_w'], 'L0_attn_v_conv_w': _L0_attn_in['v_conv_w'], 'L0_attn_f_w1': _L0_attn_in['f_w1'], 'L0_attn_f_w2': _L0_attn_in['f_w2'], 'L0_attn_b_w': _L0_attn_in['b_w'], 'L0_attn_A_log': _L0_attn_in['A_log'], 'L0_attn_dt_bias': _L0_attn_in['dt_bias'], 'L0_attn_g_w1': _L0_attn_in['g_w1'], 'L0_attn_g_w2': _L0_attn_in['g_w2'], 'L0_attn_g_b2': _L0_attn_in['g_b2'], 'L0_attn_o_norm_w': _L0_attn_in['o_norm_w'], 'L0_attn_o_w': _L0_attn_in['o_w'], 'L0_ffn_Wr': _L0_ffn_in['Wr'], 'L0_ffn_bias': _L0_ffn_in['bias'], 'L0_ffn_Wg': _L0_ffn_in['Wg'], 'L0_ffn_Wu': _L0_ffn_in['Wu'], 'L0_ffn_Wd': _L0_ffn_in['Wd'], 'L0_ffn_sWg': _L0_ffn_in['sWg'], 'L0_ffn_sWu': _L0_ffn_in['sWu'], 'L0_ffn_sWd': _L0_ffn_in['sWd']}
    _x0 = _d['L0_attn_hidden_states']
    _d['L0_attn_hidden_states'] = jax.random.normal(jax.random.fold_in(jax.random.key(seed), 1), (4, 1024, 256), dtype=_x0.dtype)
    del _x0
    return _d

def reference(L0_attn_hidden_states, L0_attn_q_w, L0_attn_k_w, L0_attn_v_w, L0_attn_q_conv_w, L0_attn_k_conv_w, L0_attn_v_conv_w, L0_attn_f_w1, L0_attn_f_w2, L0_attn_b_w, L0_attn_A_log, L0_attn_dt_bias, L0_attn_g_w1, L0_attn_g_w2, L0_attn_g_b2, L0_attn_o_norm_w, L0_attn_o_w, L0_ffn_Wr, L0_ffn_bias, L0_ffn_Wg, L0_ffn_Wu, L0_ffn_Wd, L0_ffn_sWg, L0_ffn_sWu, L0_ffn_sWd):

    def _L0_attn_ref(hidden_states, q_w, k_w, v_w, q_conv_w, k_conv_w, v_conv_w, f_w1, f_w2, b_w, A_log, dt_bias, g_w1, g_w2, g_b2, o_norm_w, o_w):
        import jax, jax.numpy as jnp
        import numpy as np
        EPS_NORM = 1e-05
        EPS_L2 = 1e-06
        CHUNK = 128

        def _short_conv(x, w):
            K = w.shape[1]
            T = x.shape[1]
            xp = jnp.pad(x, ((0, 0), (K - 1, 0), (0, 0)))
            y = sum((xp[:, i:i + T, :] * w[:, i] for i in range(K)))
            return jax.nn.silu(y)

        def _l2norm(x):
            return x * jax.lax.rsqrt(jnp.sum(x * x, axis=-1, keepdims=True) + EPS_L2)

        def _kda_scan(q, k, v, gk, beta):
            B, T, H, Dk = q.shape
            Dv = v.shape[-1]
            NC = T // CHUNK

            def c4(x):
                return jnp.transpose(x.reshape(B, NC, CHUNK, H, x.shape[-1]), (1, 2, 0, 3, 4))
            qc, kc, vc, gc = (c4(q), c4(k), c4(v), c4(gk))
            bc = jnp.transpose(beta.reshape(B, NC, CHUNK, H), (1, 2, 0, 3))

            def step(S, inp):
                q_t, k_t, v_t, g_t, b_t = inp
                S = S * jnp.exp(g_t)[..., None]
                err = v_t - jnp.einsum('bhk,bhkv->bhv', k_t, S)
                S = S + b_t[..., None, None] * (k_t[..., None] * err[..., None, :])
                o_t = jnp.einsum('bhk,bhkv->bhv', q_t, S)
                return (S, o_t)

            @jax.checkpoint
            def chunk_fn(S, xs):
                return jax.lax.scan(step, S, xs)
            S0 = jnp.zeros((B, H, Dk, Dv), q.dtype)
            _, o = jax.lax.scan(chunk_fn, S0, (qc, kc, vc, gc, bc))
            return jnp.transpose(o.reshape(T, B, H, Dv), (1, 0, 2, 3))

        def _forward(hidden_states, q_w, k_w, v_w, q_conv_w, k_conv_w, v_conv_w, f_w1, f_w2, b_w, A_log, dt_bias, g_w1, g_w2, g_b2, o_norm_w, o_w):
            B, T, D = hidden_states.shape
            H = A_log.shape[0]
            Dv = o_norm_w.shape[0]
            Dk = q_w.shape[1] // H
            q = _short_conv(hidden_states @ q_w, q_conv_w).reshape(B, T, H, Dk)
            k = _short_conv(hidden_states @ k_w, k_conv_w).reshape(B, T, H, Dk)
            v = _short_conv(hidden_states @ v_w, v_conv_w).reshape(B, T, H, Dv)
            g = (hidden_states @ f_w1 @ f_w2).reshape(B, T, H, Dk)
            gk = -jnp.exp(A_log)[:, None] * jax.nn.softplus(g + dt_bias.reshape(H, Dk))
            beta = jax.nn.sigmoid(hidden_states @ b_w)
            q = _l2norm(q) * Dk ** (-0.5)
            k = _l2norm(k)
            o = _kda_scan(q, k, v, gk, beta)
            gate = (hidden_states @ g_w1 @ g_w2 + g_b2).reshape(B, T, H, Dv)
            o = o * jax.lax.rsqrt(jnp.mean(o * o, axis=-1, keepdims=True) + EPS_NORM) * o_norm_w
            o = o * jax.nn.sigmoid(gate)
            return o.reshape(B, T, H * Dv) @ o_w
        return _forward(hidden_states, q_w, k_w, v_w, q_conv_w, k_conv_w, v_conv_w, f_w1, f_w2, b_w, A_log, dt_bias, g_w1, g_w2, g_b2, o_norm_w, o_w)

    def _L0_ffn_ref(x, Wr, bias, Wg, Wu, Wd, sWg, sWu, sWd):
        import jax, jax.numpy as jnp
        import numpy as np
        TOPK = 2
        NORM_TOPK = True
        SCALE = 1.0
        EPS = 1e-09
        b, s, h = x.shape
        E = Wr.shape[0]
        xt = x.reshape(b * s, h)
        logits = xt @ Wr.T + bias
        probs = jax.nn.softmax(logits, axis=-1)
        topk_val, topk_idx = jax.lax.top_k(probs, TOPK)
        if NORM_TOPK:
            w = topk_val / (jnp.sum(topk_val, axis=-1, keepdims=True) + EPS)
        else:
            w = topk_val
        w = w * SCALE
        g = jnp.einsum('th,ehi->tei', xt, Wg)
        u = jnp.einsum('th,ehi->tei', xt, Wu)
        y = jnp.einsum('tei,eih->teh', jax.nn.silu(g) * u, Wd)
        oh = jax.nn.one_hot(topk_idx, E, dtype=x.dtype)
        routed = jnp.einsum('tke,tk,teh->th', oh, w, y)
        shared = jax.nn.silu(xt @ sWg) * (xt @ sWu) @ sWd
        return (routed + shared).reshape(b, s, h)
    x = L0_attn_hidden_states
    x = _layernorm(x + _L0_attn_ref(x, L0_attn_q_w, L0_attn_k_w, L0_attn_v_w, L0_attn_q_conv_w, L0_attn_k_conv_w, L0_attn_v_conv_w, L0_attn_f_w1, L0_attn_f_w2, L0_attn_b_w, L0_attn_A_log, L0_attn_dt_bias, L0_attn_g_w1, L0_attn_g_w2, L0_attn_g_b2, L0_attn_o_norm_w, L0_attn_o_w), axis=-1)
    x = _layernorm(x + _L0_ffn_ref(x, L0_ffn_Wr, L0_ffn_bias, L0_ffn_Wg, L0_ffn_Wu, L0_ffn_Wd, L0_ffn_sWg, L0_ffn_sWu, L0_ffn_sWd), axis=-1)
    return x

_drawn_inputs = setup_inputs


def setup_inputs(seed=0):
    import zlib

    import numpy as np

    out = dict(_drawn_inputs(seed))
    spreads = {'L0_attn_dt_bias': (0.0, 0.8),
     'L0_attn_g_b2': (0.0, 0.8),
     'L0_attn_o_norm_w': (1.0, 0.6),
     'L0_ffn_bias': (0.0, 0.8)}
    factors = {'L0_attn_q_w': 8.0,
     'L0_attn_k_w': 8.0,
     'L0_attn_v_w': 8.0,
     'L0_attn_q_conv_w': 8.0,
     'L0_attn_k_conv_w': 8.0,
     'L0_attn_v_conv_w': 8.0,
     'L0_attn_f_w1': 8.0,
     'L0_attn_f_w2': 8.0,
     'L0_attn_b_w': 8.0,
     'L0_attn_A_log': 8.0,
     'L0_attn_g_w1': 8.0,
     'L0_attn_g_w2': 8.0,
     'L0_attn_o_w': 8.0,
     'L0_ffn_Wr': 7.266,
     'L0_ffn_Wg': 6.737,
     'L0_ffn_Wu': 6.673,
     'L0_ffn_Wd': 6.668,
     'L0_ffn_sWg': 4.856,
     'L0_ffn_sWu': 4.753,
     'L0_ffn_sWd': 4.774}
    for name, (base, spread) in spreads.items():
        noise = np.random.default_rng([zlib.crc32(name.encode()), seed]).standard_normal(out[name].shape)
        drawn = base * np.exp(spread * noise) if base else spread * noise
        out[name] = jnp.asarray(drawn.astype(out[name].dtype))
    for name, factor in factors.items():
        out[name] = (out[name] * factor).astype(out[name].dtype)
    return out
```

```python
from contextlib import ExitStack

import numpy as np

import concourse.bass as bass
from concourse import mybir

FP = mybir.dt.float32
U32 = mybir.dt.uint32
ALU = mybir.AluOpType
ACT = mybir.ActivationFunctionType

B, T, D = 4, 1024, 256
H, DK = 16, 128
P = 128
KT = D // P
NCH = T // P
TAPS = 4
HALO = TAPS - 1
W = P + HALO
LEVELS = 7
HALF = P // 2
PRIMED = 1
E = 16
I = 128
EPS_NORM, EPS_L2, EPS_TOPK, EPS_LN = 1e-5, 1e-6, 1e-9, 1e-5


def build(nc, a, out):
    ctx = ExitStack()
    with ctx:
        def sb(name, shape, dt=FP):
            return ctx.enter_context(nc.sbuf_tensor(name, shape, dt))

        def ps(name):
            return ctx.enter_context(nc.psum_tensor(name, [P, 512], FP))

        def sem(name):
            return ctx.enter_context(nc.semaphore(name))

        def sems(name, n):
            return [sem(f"{name}{k}") for k in range(n)]

        XT = KT * (NCH + 1) * B * W
        XF = NCH * B * P
        arena = sb("arena", [P, XT + 2 * XF])
        xT = arena[:, 0:XT].rearrange("p (k c b w) -> p k c b w", k=KT, c=NCH + 1, b=B)
        xf = arena[:, XT:XT + XF].rearrange("p (c n) -> p c n", c=NCH)
        xg = arena[:, XT + XF:XT + 2 * XF].rearrange("p (c n) -> p c n", c=NCH)
        wgu = arena[:, 0:KT * (E + 1) * 2 * I].rearrange("p (k e n) -> p k e n", k=KT, e=E + 1)
        wdn = arena[:, KT * (E + 1) * 2 * I:(KT * 2 * I + D) * (E + 1)].rearrange("p (e n) -> p e n", e=E + 1)
        acc = sb("acc", [P, NCH, B, D])
        ow = sb("ow", [P, H, D])
        wqkv = sb("wqkv", [P, 3, KT, DK])
        wf2 = sb("wf2", [P, DK])
        wg2 = sb("wg2", [P, DK])
        convw = sb("convw", [P, 3, H + 1, TAPS])
        dtb = sb("dtb", [P, H + 1])
        gb2h = sb("gb2h", [P, H + 1])
        negA = sb("negA", [P, H + 1])
        beta = sb("beta", [P, H + 1, NCH, B])
        onw = sb("onw", [P, 1])
        ident = sb("ident", [P, P])
        ones = sb("ones", [P, 1])
        keep = sb("keep", [P, NCH])
        mhalf = sb("mhalf", [P, 16])
        mask = sb("mask", [P, LEVELS, HALF])
        qkd = sb("qkd", [P, 4, B, P])
        pre = sb("pre", [P, 2, B, P])
        sq = sb("sq", [P, 2, B, P])
        fsp = sb("fsp", [P, 4, B, P])
        FQ = sb("FQ", [P, 2, B, P])
        KR = sb("KR", [P, B, P])
        PB = sb("PB", [P, B * (P - 1)])
        NT = sb("NT", [P, LEVELS, B, P])
        XL = sb("XL", [P, LEVELS, B, P])
        TM = sb("TM", [P, B, P])
        TT = sb("TT", [P, B, P])
        AT = sb("AT", [P, B, P])
        R = sb("R", [P, B, P])
        U = sb("U", [P, B, P])
        KRt = sb("KRt", [P, B, P])
        S = sb("S", [P, B, P])
        gt = sb("gt", [P, B, P])
        G = sb("G", [P, B, P])
        onesrow, alog = KRt[0:1, 0], KRt[0:1, 1, 0:H]
        nxt = sb("nxt", [P, 4, B])
        cur = sb("cur", [P, 4, B])
        ssum = sb("ssum", [P, 2, B])
        sinv = sb("sinv", [P, 2, B])
        rr = sb("rr", [P, 3, B])
        flatN = NT[:].rearrange("p l b n -> p (l b n)")
        flatZ = XL[:].rearrange("p l b n -> p (l b n)")
        xn = flatN[:, 0:1024].rearrange("p (b n) -> p b n", b=B)
        x1 = flatN[:, 1024:2048].rearrange("p (b n) -> p b n", b=B)
        x1T = flatN[:, 2048:3072].rearrange("p (k n) -> p k n", k=KT)
        yo = flatZ[:, 0:1024].rearrange("p (b n) -> p b n", b=B)
        sg = [flatZ[:, 1024 + 512 * s:1536 + 512 * s].rearrange("p (b n) -> p b n", b=B) for s in range(2)]
        hw = [qkd[:, s] for s in range(2)]
        hT = [qkd[:, 2 + s] for s in range(2)]
        scrap = sb("scrap", [P, 1])
        stats = sb("stats", [P, B, 6])
        mv = sb("mv", [P, B, 2])
        rstd = sb("rstd", [P, B])
        wrn = G[0:E, 0:2].rearrange("p a n -> p (a n)")
        wrT = sb("wrT", [P, KT, E])
        rbias = sb("rbias", [P, E])
        logit = AT[:, 0, 0:B * E].rearrange("p (b e) -> p b e", b=B)
        nmax = sb("nmax", [P, B])
        den = sb("den", [P, 2, B])
        top, topi, topf = (AT[:, 2, 8 * B * x:8 * B * (x + 1)].rearrange("p (b n) -> p b n", b=B) for x in range(3))
        topi = topi.bitcast(U32)
        tsum = sb("tsum", [P, B])
        tw = sb("tw", [P, B, 2])
        iot = sb("iot", [P, E])
        wsel = AT[:, 1, 0:2 * B * E].rearrange("p (x b e) -> p x b e", x=2, b=B)
        wexp = sb("wexp", [P, E + 1, B])

        pj = ctx.enter_context(nc.psum_tensor("pj", [P, 2, 2, 512], FP))
        b4, b5, b6, b7 = ps("b4"), ps("b5"), ps("b6"), ps("b7")
        pair = [pj[:, n].rearrange("p a (x w) -> p (a x) w", x=2) for n in range(2)]
        xnat = pre[:].rearrange("p a b n -> p (a b n)").rearrange("p (b n) -> p b n", b=B)
        xs = fsp[:, 0:2].rearrange("p a b n -> p (a b n)")
        gu = pair
        bank_f, bank_g = pj[:, 1, 0], pj[:, 1, 1]
        sums_qk = pj[:, 0, 0, 0:2 * B].rearrange("p (x b) -> p x b", x=2)

        def quad(bank):
            return bank[:, 0:512].rearrange("p (b n) -> p b n", b=B)

        def halves(ap, n):
            v = ap.rearrange("p b (m two n) -> p b m two n", two=2, n=n)
            return v[:, :, :, 0, :], v[:, :, :, 1, :]

        def part(bank, lo, n):
            return bank[:, lo:lo + B * HALF].rearrange("p (b m n) -> p b m n", b=B, n=n)

        s_const = sem("s_const")
        s_chain = {k: sem(f"s_chain_{k}") for k in ("pool", "dve", "act")}
        s_ld = sem("s_ld")
        s_xin, s_xtr, s_xcp, s_xtc, s_xfm, s_xfc = (sem(n) for n in ("s_xin", "s_xtr", "s_xcp", "s_xtc", "s_xfm", "s_xfc"))
        s_bm, s_bc, s_apm = sem("s_bm"), sem("s_bc"), sem("s_apm")
        w_loaded = sems("w_loaded", 5)
        proj_done = sems("proj_done", 5)
        tap_done = sems("tap_done", 3)
        conv_step = sems("conv_step", 3)
        conv_done = sems("conv_done", 3)
        silu_done = sems("silu_done", 3)
        sq_done = sems("sq_done", 2)
        sums_done, sums_read, inv_done, nxt1, nxt_done, cur_done = (
            sem(n) for n in ("sums_done", "sums_read", "inv_done", "nxt1", "nxt_done", "cur_done"))
        f_abs, f_relu, f_exp, f_ln, f_w1, f_sub, f_add, f_sum, d_exp, d_done, gate_done = (
            sem(n) for n in ("f_abs", "f_relu", "f_exp", "f_ln", "f_w1", "f_sub", "f_add", "f_sum", "d_exp", "d_done", "gate_done"))
        init_done, tt_init, diag_done, vt_done, at_init, vp_done = (
            sem(n) for n in ("init_done", "tt_init", "diag_done", "vt_done", "at_init", "vp_done"))
        x_mm, x_done, t_mm, t_add, kr_init = (sem(n) for n in ("x_mm", "x_done", "t_mm", "t_add", "kr_init"))
        lvl_mm = sem("lvl_mm")
        blk_done = sem("blk_done")
        lvl_upd = sem("lvl_upd")
        kk_done = sem("kk_done")
        qk_done = sem("qk_done")
        tt_mm = sem("tt_mm")
        tt_add = sem("tt_add")
        krt_mm, krt_done, y_mm, r_done, u_mm, u_done, o_mm, s_mm, s_done = (
            sem(n) for n in ("krt_mm", "krt_done", "y_mm", "r_done", "u_mm", "u_done", "o_mm", "s_mm", "s_done"))
        g_done, o2_done, osum_mm, ms_done, ms_eps, ms_pow, r_ready, out_mm, acc_done = (
            sem(n) for n in ("g_done", "o2_done", "osum_mm", "ms_done", "ms_eps", "ms_pow", "r_ready", "out_mm", "acc_done"))
        m_w = sem("m_w")
        (m_x, m_y, m_st, m_ag, m_ep, m_rs, m_x1, m_tr, m_xT, m_lg, m_lb, m_mx, m_nm, m_ex, m_de, m_rc, m_pr, m_tp, m_ti, m_tf,
         m_ts, m_te, m_tr2, m_tw, m_s0, m_s1, m_we, m_seed, m_fin, m_s2, m_st2, m_ag2, m_ep2, m_rs2, m_yo, m_out) = (
            sem(n) for n in ("m_x m_y m_st m_ag m_ep m_rs m_x1 m_tr m_xT m_lg m_lb m_mx m_nm m_ex m_de m_rc m_pr m_tp m_ti m_tf "
                             "m_ts m_te m_tr2 m_tw m_s0 m_s1 m_we m_seed m_fin m_s2 m_st2 m_ag2 m_ep2 m_rs2 m_yo m_out").split())
        gu_mm, silu_e, h_e, ht_mm, ht_e, dn_mm = (sem(n) for n in ("gu_mm", "silu_e", "h_e", "ht_mm", "ht_e", "dn_mm"))

        def wait(eng, s, value):
            if isinstance(value, int) and value <= 0:
                return
            eng.wait_ge(s, value)

        def upto(l, i, first=0):
            return i * (LEVELS - first) + (l - first + 1)

        def over_quads(eng, stage_a, body):
            stage_a(0, 0, 0)
            with eng.Fori(0, H) as h:
                with eng.Fori(0, NCH - 1) as c:
                    body(h * NCH + c, h, c, h, c + 1)
                body(h * NCH + (NCH - 1), h, NCH - 1, h + 1, 0)

        def bcast(ap, shape):
            return ap.to_broadcast(shape)

        block = ctx.enter_context(nc.Block())
        names = ("q", "k", "v")

        @block.sync
        def _(sp):
            for s in (o_mm, r_ready, acc_done, s_done, o2_done, osum_mm, s_bm, s_xcp, s_xfc, s_bc, m_seed, m_s2, m_out,
                      h_e, ht_e, ht_mm):
                sp.sem_inc(s, PRIMED)
            n = 0
            for dst, src in (
                (convw[:, 0, 0:H], a["q_conv_w"].rearrange("(h p) t -> p h t", p=P)),
                (convw[:, 1, 0:H], a["k_conv_w"].rearrange("(h p) t -> p h t", p=P)),
                (convw[:, 2, 0:H], a["v_conv_w"].rearrange("(h p) t -> p h t", p=P)),
                (dtb[:, 0:H], a["dt_bias"].rearrange("(h p) -> p h", p=P)),
                (gb2h[:, 0:H], a["g_b2"].rearrange("(h p) -> p h", p=P)),
                (alog, a["A_log"].rearrange("(o h) -> o h", o=1)),
                (onw[:], a["o_norm_w"].rearrange("(p o) -> p o", o=1)),
                (ow[:], a["o_w"].rearrange("(h p) n -> p h n", p=P)),
                (wrn, a["Wr"]),
                (R[:, 0:2], a["f_w1"].rearrange("(k p) n -> p k n", p=P)),
                (R[:, 2:4], a["g_w1"].rearrange("(k p) n -> p k n", p=P)),
                (U[:, 0, 0:KT * H].rearrange("p (k h) -> p k h", k=KT), a["b_w"].rearrange("(k p) n -> p k n", p=P)),
                (rbias[:], a["bias"].partition_broadcast(P)),
            ):
                sp.dma_start(dst, src, allow_slow_non_contiguous=True).then_inc(s_ld, 16)
                n += 1

            def weights(h, prev):
                for x, name in enumerate(("q_w", "k_w", "v_w")):
                    wait(sp, proj_done[x], prev)
                    sp.dma_start(wqkv[:, x], a[name].rearrange("(k p) (h n) -> p k h n", p=P, n=DK)[:, :, h, :]
                                 ).then_inc(w_loaded[x], 16)
                for x, (dst, name) in enumerate(((wf2, "f_w2"), (wg2, "g_w2"))):
                    wait(sp, proj_done[3 + x], prev)
                    sp.dma_start(dst[:], a[name].rearrange("p (h n) -> p h n", n=DK)[:, h, :]).then_inc(w_loaded[3 + x], 16)

            xsrc = a["x"].rearrange("b (c p) d -> p c b d", p=P)
            sp.dma_start(xnat, xsrc[:, 0]).then_inc(s_xin, 16)
            weights(0, 0)
            with sp.Fori(1, NCH) as c:
                sp.wait_ge(s_xtr, c)
                sp.dma_start(xnat, xsrc[:, c]).then_inc(s_xin, 16)
            with sp.Fori(1, H) as h:
                weights(h, h * NCH)
            weights(0, H * NCH)

            sp.wait_ge(proj_done[4], H * NCH + 1)
            for k in range(KT):
                for x, (name, shared) in enumerate((("Wg", "sWg"), ("Wu", "sWu"))):
                    sp.dma_start(wgu[:, k, 0:E, x * I:(x + 1) * I],
                                 a[name].rearrange("e (k p) n -> p k e n", p=P)[:, k]).then_inc(m_w, 16)
                    sp.dma_start(wgu[:, k, E, x * I:(x + 1) * I],
                                 a[shared].rearrange("(k p) n -> p k n", p=P)[:, k]).then_inc(m_w, 16)
            sp.dma_start(wdn[:, 0:E], a["Wd"].rearrange("e p n -> p e n")).then_inc(m_w, 16)
            sp.dma_start(wdn[:, E], a["sWd"]).then_inc(m_w, 16)
            sp.wait_ge(out_mm, H * NCH)
            odst = out.rearrange("b (c p) d -> p c b d", p=P)
            sp.dma_start(xn, xsrc[:, 0]).then_inc(m_x, 16)

            def store(g):
                sp.wait_ge(m_yo, (g + 1) * B)
                sp.dma_start(odst[:, g], yo).then_inc(m_out, 16)

            with sp.Fori(0, NCH - 1) as g:
                sp.wait_ge(m_y, g + 1)
                sp.dma_start(xn, xsrc[:, g + 1]).then_inc(m_x, 16)
                store(g)
            store(NCH - 1)
            sp.wait_ge(m_out, PRIMED + 16 * NCH)

        @block.gpsimd
        def _(pool):
            cnt = [0]

            def link(ins):
                cnt[0] += 1
                ins.then_inc(s_chain["pool"], 1)
                pool.wait_ge(s_chain["pool"], cnt[0])

            for t, v in ((ident[:], 0.0), (ones[:], 1.0), (onesrow, 1.0), (keep[:], 1.0), (mhalf[:], -0.5),
                         (mask[:], 1.0), (NT[:], 0.0), (XL[:], 0.0), (S[:], 0.0),
                         (xT[:, :, 0, :, 0:HALO], 0.0), (convw[:, :, H], 0.0), (dtb[:, H:H + 1], 0.0),
                         (gb2h[:, H:H + 1], 0.0), (negA[:, H:H + 1], 0.0), (beta[:, H], 0.0), (wexp[:, E], 1.0)):
                link(nc.gpsimd.memset(t, v))
            link(nc.gpsimd.memset(keep[:, 0:1], 0.0))
            link(nc.gpsimd.iota(topi[:, 0:2, :].rearrange("p b n -> p (b n)").bitcast(mybir.dt.int32), [[1, E]], base=0, channel_multiplier=0))
            link(nc.gpsimd.tensor_copy(iot[:], topi[:, 0:2, :].rearrange("p b n -> p (b n)").bitcast(mybir.dt.int32)))
            link(nc.gpsimd.affine_select(out=ident[:], in_=ident[:], compare_op=ALU.not_equal, fill=1.0, base=0,
                                         pattern=[[-1, P]], channel_multiplier=1))
            for l in range(LEVELS):
                n = 1 << l
                m = HALF // n
                v = mask[:, l].rearrange("p (m n) -> p m n", n=n)
                link(nc.gpsimd.affine_select(out=v, in_=v, compare_op=ALU.is_ge, fill=0.0, base=0,
                                             pattern=[[-2 * n, m], [0, n]], channel_multiplier=1))
                link(nc.gpsimd.affine_select(out=v, in_=v, compare_op=ALU.is_ge, fill=0.0, base=n - 1,
                                             pattern=[[2 * n, m], [0, n]], channel_multiplier=-1))
            nc.gpsimd.memset(acc[:], 0.0).then_inc(s_const, 1)

            def stage_a(j, h, c):
                pool.wait_ge(f_w1, j + 1)
                nc.gpsimd.tensor_tensor(fsp[:, 3], fsp[:, 1], fsp[:, 3], ALU.subtract).then_inc(f_sub, 1)
                pool.wait_ge(f_relu, j + 1)
                pool.wait_ge(f_sub, j + 1)
                nc.gpsimd.tensor_tensor(fsp[:, 3], fsp[:, 3], fsp[:, 0], ALU.add).then_inc(f_add, 1)
                pool.wait_ge(f_add, j + 1)
                pool.wait_ge(f_ln, j + 1)
                nc.gpsimd.tensor_tensor(fsp[:, 3], fsp[:, 3], fsp[:, 2], ALU.add).then_inc(f_sum, 1)

            def stage_a_cols(j, h, c):
                pool.wait_ge(sums_read, j + 1)
                nc.gpsimd.tensor_tensor(sinv[:], ssum[:], mhalf[:, 0:2 * B].rearrange("p (x b) -> p x b", x=2), ALU.pow
                                        ).then_inc(inv_done, 1)
                pool.wait_ge(inv_done, j + 1)
                wait(pool, cur_done, j)
                nc.gpsimd.tensor_tensor(nxt[:, 0], sinv[:, 1], beta[:, h, c, :], ALU.mult).then_inc(nxt1, 1)
                nc.gpsimd.tensor_tensor(nxt[:, 3], sinv[:, 0], sinv[:, 0], ALU.mult)
                nc.gpsimd.tensor_copy(nxt[:, 2], sinv[:, 0])
                pool.wait_ge(nxt1, j + 1)
                nc.gpsimd.tensor_tensor(nxt[:, 1], nxt[:, 0], sinv[:, 1], ALU.mult).then_inc(nxt_done, 1)

            def stage_a_keep(j, h, c):
                pool.wait_ge(d_exp, j + 1)
                nc.gpsimd.tensor_tensor(qkd[:, 3, :, 0], qkd[:, 3, :, 0], bcast(keep[:, bass.ds(c, 1)], [P, B]), ALU.mult
                                        ).then_inc(d_done, 1)

            def prologue(j, h, c):
                pool.wait_ge(s_bc, PRIMED + NCH)
                stage_a(j, h, c)
                stage_a_keep(j, h, c)
                stage_a_cols(j, h, c)

            off = [0]
            for l in range(LEVELS):
                off.append(off[-1] + B * (HALF >> l))

            def blocks(l):
                if l == 0:
                    return qkd[:, 3].rearrange("p b n -> p (b n)")
                return PB[:, off[l - 1]:off[l]]

            def body(i, h, c, hn, cn):
                pool.wait_ge(silu_done[1], i + 1)
                pool.wait_ge(o_mm, PRIMED + i)
                pool.wait_ge(d_done, i + 1)
                nc.gpsimd.tensor_tensor(FQ[:, 0], qkd[:, 1], qkd[:, 3], ALU.mult)
                pool.wait_ge(silu_done[0], i + 1)
                nc.gpsimd.tensor_tensor(FQ[:, 1], qkd[:, 0], qkd[:, 3], ALU.mult).then_inc(init_done, 1)

                for l in range(LEVELS):
                    n = 1 << l
                    pl = blocks(l).rearrange("p (m two) -> p m two", two=2)
                    if l:
                        pool.wait_ge(blk_done, upto(l - 1, i))
                    nc.gpsimd.tensor_tensor(blocks(l + 1), pl[:, :, 0], pl[:, :, 1], ALU.mult).then_inc(blk_done, 1)
                    pool.wait_ge(lvl_mm, upto(l, i))
                    if l == 0:
                        pool.wait_ge(init_done, i + 1)
                    else:
                        pool.wait_ge(lvl_upd, upto(l - 1, i))
                    kl, _ = halves(KR[:], n)
                    kl = kl.rearrange("p b m n -> p (b m) n")
                    nc.gpsimd.tensor_tensor(kl, kl, bcast(pl[:, :, 1:2], [P, B * HALF // n, n]), ALU.mult)
                    fr = FQ[:].rearrange("p x b (m two n) -> p x (b m) two n", two=2, n=n)[:, :, :, 1, :]
                    nc.gpsimd.tensor_tensor(fr, fr, bcast(pl[:, :, 0:1].unsqueeze(1), [P, 2, B * HALF // n, n]), ALU.mult
                                            ).then_inc(lvl_upd, 1)
                    if l == 1:
                        stage_a(i + 1, hn, cn)
                    if l == 3:
                        stage_a_keep(i + 1, hn, cn)
                stage_a_cols(i + 1, hn, cn)
                pool.wait_ge(ms_eps, i + 1)
                nc.gpsimd.tensor_tensor(rr[:, 1], rr[:, 0], mhalf[:, 0:B], ALU.pow).then_inc(ms_pow, 1)
                pool.wait_ge(ms_pow, i + 1)
                nc.gpsimd.tensor_tensor(rr[:, 2], rr[:, 1], cur[:, 2], ALU.mult).then_inc(r_ready, 1)

            over_quads(pool, prologue, body)

            with pool.Fori(0, NCH) as g:
                pool.wait_ge(m_ep, g + 1)
                nc.gpsimd.tensor_tensor(rstd[:], rstd[:], mhalf[:, 0:B], ALU.pow).then_inc(m_rs, 1)
                pool.wait_ge(m_ep2, g + 1)
                nc.gpsimd.tensor_tensor(rstd[:], rstd[:], mhalf[:, 0:B], ALU.pow).then_inc(m_rs2, 1)

        @block.scalar
        def _(act):
            act.wait_ge(s_ld, 16 * 13)
            act.wait_ge(s_const, 1)
            nc.scalar.mul(gb2h[:, 0:H], gb2h[:, 0:H], 0.5)
            act.wait_ge(s_apm, 1)
            nc.scalar.activation(negA[:, 0:H], b4[:, 0:H], ACT.Exp).then_inc(s_chain["act"], 1)
            act.wait_ge(s_chain["act"], 1)
            nc.scalar.mul(negA[:, 0:H], negA[:, 0:H], -1.0).then_inc(s_chain["act"], 1)
            nc.scalar.copy(wrT[:], b4[:, 64:64 + KT * E].rearrange("p (k e) -> p k e", k=KT)).then_inc(s_chain["act"], 1)
            nc.scalar.mul(ow[:], ow[:], onw[:]).then_inc(s_chain["act"], 1)
            act.wait_ge(s_chain["act"], 4)

            with act.Fori(0, NCH) as c:
                act.wait_ge(s_xtr, c + 1)
                act.wait_ge(s_bm, PRIMED + c)
                nc.scalar.copy(xs, pj[:, 0].rearrange("p a n -> p (a n)")).then_inc(s_xcp, 1)
                act.wait_ge(s_xfm, c + 1)
                nc.scalar.copy(xf[:, c], b5[:])
                nc.scalar.copy(xg[:, c], b6[:]).then_inc(s_xfc, 1)
                act.wait_ge(s_bm, PRIMED + c + 1)
                nc.scalar.activation(beta[:, 0:H, c, :].rearrange("p h b -> p b h"),
                                     b7[:, 0:B * H].rearrange("p (b h) -> p b h", b=B), ACT.Sigmoid).then_inc(s_bc, 1)

            def tap(x, j, h):
                act.wait_ge(proj_done[x], j + 1)
                if x == 2:
                    act.wait_ge(silu_done[0], j + 1)
                elif x == 0:
                    wait(act, silu_done[2], j)
                else:
                    wait(act, silu_done[1], j)
                nc.scalar.activation(pre[:, x % 2], pair[x % 2][:, :, 0:P], ACT.Copy, scale=convw[:, x, h, 0:1]
                                     ).then_inc(tap_done[x], 1)

            def silu(x, j):
                act.wait_ge(conv_done[x], j + 1)
                wait(act, init_done, j)
                wait(act, vt_done, j)
                nc.scalar.activation(qkd[:, x], pre[:, x % 2], ACT.Silu).then_inc(silu_done[x], 1)

            def square(x, j):
                act.wait_ge(silu_done[x], j + 1)
                wait(act, sums_done, j)
                if x == 0:
                    wait(act, osum_mm, PRIMED + j - 1)
                nc.scalar.activation(sq[:, x], qkd[:, x], ACT.Square).then_inc(sq_done[x], 1)

            def f_start(j, h):
                act.wait_ge(proj_done[3], j + 1)
                wait(act, f_sum, j)
                f = quad(bank_f)
                nc.scalar.activation(fsp[:, 1], f, ACT.Abs, bias=dtb[:, bass.ds(h, 1)]).then_inc(f_abs, 1)
                nc.scalar.activation(fsp[:, 0], f, ACT.Relu, bias=dtb[:, bass.ds(h, 1)]).then_inc(f_relu, 1)

            def f_e(j):
                act.wait_ge(f_abs, j + 1)
                nc.scalar.activation(fsp[:, 1], fsp[:, 1], ACT.Exp, scale=-1.0).then_inc(f_exp, 1)

            def f_l(j):
                act.wait_ge(f_exp, j + 1)
                nc.scalar.activation(fsp[:, 2], fsp[:, 1], ACT.Ln, bias=1.0).then_inc(f_ln, 1)

            def f_d(j, h):
                act.wait_ge(f_sum, j + 1)
                wait(act, lvl_upd, upto(0, j - 1))
                wait(act, blk_done, upto(0, j - 1))
                nc.scalar.activation(qkd[:, 3], fsp[:, 3], ACT.Exp, scale=negA[:, bass.ds(h, 1)]).then_inc(d_exp, 1)

            def gate(j, h):
                act.wait_ge(proj_done[4], j + 1)
                wait(act, g_done, j)
                nc.scalar.activation(gt[:], quad(bank_g), ACT.Tanh, bias=gb2h[:, bass.ds(h, 1)], scale=0.5).then_inc(gate_done, 1)

            def prologue(j, h, c):
                f_start(j, h)
                f_e(j)
                f_l(j)
                tap(0, j, h)
                f_d(j, h)
                tap(1, j, h)
                silu(0, j)
                square(0, j)
                tap(2, j, h)
                silu(1, j)
                square(1, j)
                silu(2, j)
                gate(j, h)

            def body(i, h, c, hn, cn):
                j = i + 1

                f_start(j, hn)
                f_e(j)
                f_l(j)
                tap(0, j, hn)
                f_d(j, hn)
                tap(1, j, hn)
                silu(0, j)
                square(0, j)
                silu(1, j)
                square(1, j)
                act.wait_ge(krt_mm, i + 1)
                nc.scalar.copy(KRt[:], quad(b4)).then_inc(krt_done, 1)
                tap(2, j, hn)
                silu(2, j)
                act.wait_ge(u_mm, i + 1)
                nc.scalar.copy(U[:], quad(b5)).then_inc(u_done, 1)
                act.wait_ge(g_done, i + 1)
                act.wait_ge(sums_done, j + 1)
                nc.scalar.activation(sq[:, 0], quad(b6), ACT.Square).then_inc(o2_done, 1)
                gate(j, hn)

            over_quads(act, prologue, body)

            with act.Fori(0, NCH) as g:
                act.wait_ge(m_tr, g + 1)
                nc.scalar.copy(x1T, pj[:, 0].rearrange("p a n -> p (a n)").rearrange("p (k n) -> p k n", k=KT)).then_inc(m_xT, 1)
                act.wait_ge(m_nm, g + 1)
                for b in range(B):
                    nc.scalar.activation(logit[:, b], logit[:, b], ACT.Exp, bias=nmax[:, b:b + 1],
                                         accum_out=den[:, 0, b:b + 1]).then_inc(m_ex, 1)

                n0 = g * (E + 1)
                act.wait_ge(gu_mm, n0 + 1)
                act.wait_ge(h_e, PRIMED + n0)
                nc.scalar.activation(sg[0], gu[0][:, :, 0:I], ACT.Silu).then_inc(silu_e, 1)
                with act.Fori(0, E // 2) as e2:
                    for s in range(2):
                        n = n0 + e2 * 2 + s
                        act.wait_ge(gu_mm, n + 2)
                        act.wait_ge(h_e, PRIMED + n)
                        nc.scalar.activation(sg[1 - s], gu[1 - s][:, :, 0:I], ACT.Silu).then_inc(silu_e, 1)
                        act.wait_ge(ht_mm, PRIMED + n + 1)
                        nc.scalar.copy(hT[s], quad(b4)).then_inc(ht_e, 1)
                act.wait_ge(ht_mm, PRIMED + n0 + E + 1)
                nc.scalar.copy(hT[0], quad(b4)).then_inc(ht_e, 1)

        @block.vector
        def _(dve):
            with dve.Fori(0, NCH) as c:
                dve.wait_ge(s_xcp, PRIMED + c + 1)
                v = xs.rearrange("p (k b n) -> p k b n", k=KT, b=B)
                for k in range(KT):
                    nc.vector.tensor_copy(xT[:, k, c, :, HALO:W], v[:, k])
                    ins = nc.vector.tensor_copy(xT[:, k, c + 1, :, 0:HALO], v[:, k, :, P - HALO:P])
                ins.then_inc(s_xtc, 1)

            def conv(x, j, h, taps=range(1, TAPS)):
                src = pair[x % 2]
                for t in taps:
                    if t == 1:
                        dve.wait_ge(tap_done[x], j + 1)
                    else:
                        dve.wait_ge(conv_step[x], 2 * j + t - 1)
                    nc.vector.scalar_tensor_tensor(
                        pre[:, x % 2], src[:, :, t:t + P], convw[:, x, h, t:t + 1], pre[:, x % 2], ALU.mult, ALU.add
                    ).then_inc(conv_done[x] if t == HALO else conv_step[x], 1)

            def f_low(j):
                dve.wait_ge(f_exp, j + 1)
                wait(dve, d_exp, j)
                nc.vector.tensor_scalar(fsp[:, 3], fsp[:, 1], 1.0, 1.0, ALU.add, ALU.subtract).then_inc(f_w1, 1)

            def sums(j):
                dve.wait_ge(sums_done, j + 1)
                wait(dve, nxt_done, j)
                nc.vector.tensor_scalar(ssum[:, 1], sums_qk[:, 1], EPS_L2, None, ALU.add)
                nc.vector.tensor_scalar(ssum[:, 0], sums_qk[:, 0], EPS_L2, float(DK), ALU.add, ALU.mult).then_inc(sums_read, 1)

            def prologue(j, h, c):
                f_low(j)
                conv(0, j, h)
                conv(1, j, h)
                conv(2, j, h)
                sums(j)

            def body(i, h, c, hn, cn):
                j = i + 1

                def level(l):
                    n = 1 << l
                    pp = quad(b4).rearrange("p b (x m n) -> p b x m n", x=2, n=n)
                    mk = bcast(mask[:, l].rearrange("p (m n) -> p m n", n=n).unsqueeze(1), [P, B, HALF // n, n])
                    dve.wait_ge(lvl_mm, upto(l, i))
                    if l == 0:
                        dve.wait_ge(at_init, i + 1)
                    else:
                        dve.wait_ge(qk_done, upto(l - 1, i))
                    _, right = halves(NT[:, l], n)
                    nc.vector.tensor_tensor(right, pp[:, :, 0], mk, ALU.mult).then_inc(kk_done, 1)
                    _, right = halves(AT[:], n)
                    nc.vector.copy_predicated(right, mk.bitcast(U32), pp[:, :, 1]).then_inc(qk_done, 1)

                def x_scale(l):
                    n = 1 << l
                    dve.wait_ge(x_mm, upto(l, i))
                    left, _ = halves(XL[:, l], n)
                    nc.vector.tensor_tensor(left, part(b5, 0, n),
                                            bcast(cur[:, 1].unsqueeze(2).unsqueeze(3), [P, B, HALF // n, n]),
                                            ALU.mult).then_inc(x_done, 1)

                def add_t(l):
                    n = 1 << l
                    dve.wait_ge(t_mm, i * (LEVELS - 1) + l + 1)
                    if l == 0:
                        dve.wait_ge(tt_init, i + 1)
                    else:
                        dve.wait_ge(t_add, i * (LEVELS - 1) + l)
                    left, _ = halves(TM[:], n)
                    nc.vector.tensor_tensor(left, left, part(b6, 0, n), ALU.add).then_inc(t_add, 1)

                def add_tt(l):
                    n = 1 << l
                    dve.wait_ge(tt_mm, upto(l, i))
                    if l:
                        dve.wait_ge(tt_add, upto(l - 1, i))
                    _, right = halves(TT[:], n)
                    nc.vector.tensor_tensor(right, right, part(b7, 0, n), ALU.add).then_inc(tt_add, 1)

                dve.wait_ge(o_mm, PRIMED + i)
                dve.wait_ge(silu_done[1], i + 1)
                nc.vector.tensor_copy(KR[:], qkd[:, 1]).then_inc(kr_init, 1)
                nc.vector.tensor_copy(TM[:], bcast(ident[:].unsqueeze(1), [P, B, P]))
                nc.vector.tensor_copy(TT[:], bcast(ident[:].unsqueeze(1), [P, B, P])).then_inc(tt_init, 1)
                dve.wait_ge(nxt_done, i + 1)
                dve.wait_ge(r_ready, PRIMED + i)
                nc.vector.tensor_copy(cur[:, 0], nxt[:, 0])
                nc.vector.tensor_scalar(cur[:, 1], nxt[:, 1], -1.0, None, ALU.mult)
                nc.vector.tensor_scalar(cur[:, 2], nxt[:, 2], 0.5, None, ALU.mult)
                nc.vector.tensor_scalar(cur[:, 3], nxt[:, 3], 1.0 / DK, None, ALU.mult).then_inc(cur_done, 1)
                dve.wait_ge(diag_done, i + 1)
                nc.vector.tensor_tensor(AT[:], quad(b7), bcast(ident[:].unsqueeze(1), [P, B, P]), ALU.mult).then_inc(at_init, 1)
                dve.wait_ge(vt_done, i + 1)
                dve.wait_ge(cur_done, i + 1)
                nc.vector.tensor_tensor(R[:], quad(b5), bcast(cur[:, 0].unsqueeze(2), [P, B, P]), ALU.mult).then_inc(vp_done, 1)
                level(0)
                level(1)
                x_scale(0)
                f_low(j)
                add_t(0)
                level(2)
                add_tt(0)
                x_scale(1)
                add_t(1)
                level(3)
                add_tt(1)
                conv(0, j, hn, (1,))
                x_scale(2)
                conv(0, j, hn, (2,))
                add_t(2)
                level(4)
                add_tt(2)
                conv(0, j, hn, (3,))
                x_scale(3)
                add_t(3)
                level(5)
                add_tt(3)
                conv(1, j, hn, (1,))
                x_scale(4)
                conv(1, j, hn, (2,))
                add_t(4)
                level(6)
                add_tt(4)
                conv(1, j, hn, (3,))
                x_scale(5)
                add_t(5)
                add_tt(5)
                conv(2, j, hn, (1,))
                x_scale(6)
                conv(2, j, hn, (2,))
                dve.wait_ge(y_mm, i + 1)
                dve.wait_ge(vp_done, i + 1)
                for b in range(B):
                    ins = nc.vector.scalar_tensor_tensor(R[:, b], quad(b4)[:, b], cur[:, 1, b:b + 1], R[:, b], ALU.mult, ALU.add)
                ins.then_inc(r_done, 1)
                add_tt(6)
                conv(2, j, hn, (3,))
                sums(j)
                dve.wait_ge(o_mm, PRIMED + i + 1)
                dve.wait_ge(gate_done, i + 1)
                nc.vector.scalar_tensor_tensor(G[:], gt[:], 1.0, quad(b6), ALU.add, ALU.mult).then_inc(g_done, 1)
                dve.wait_ge(s_mm, i + 1)
                dve.wait_ge(lvl_upd, upto(6, i))
                dve.wait_ge(blk_done, upto(6, i))
                p128 = PB[:, B * (P - 2):B * (P - 1)]
                for b in range(B):
                    ins = nc.vector.scalar_tensor_tensor(S[:, b], S[:, b], p128[:, b:b + 1], quad(b7)[:, b], ALU.mult, ALU.add)
                ins.then_inc(s_done, 1)
                dve.wait_ge(osum_mm, PRIMED + i + 1)
                nc.vector.tensor_tensor(rr[:, 0], b5[:, 0:B], cur[:, 3], ALU.mult).then_inc(ms_done, 1)
                dve.wait_ge(ms_done, i + 1)
                nc.vector.tensor_scalar(rr[:, 0], rr[:, 0], EPS_NORM, None, ALU.add).then_inc(ms_eps, 1)
                dve.wait_ge(out_mm, i + 1)
                dve.wait_ge(r_ready, PRIMED + i + 1)
                for b in range(B):
                    bank = (b4, b6)[b // 2]
                    o = acc[:, c, b, :]
                    ins = nc.vector.scalar_tensor_tensor(o, bank[:, (b % 2) * D:(b % 2 + 1) * D], rr[:, 2, b:b + 1], o,
                                                         ALU.mult, ALU.add)
                    if b % 2:
                        ins.then_inc(acc_done, 1)

            dve.wait_ge(s_const, 1)
            over_quads(dve, prologue, body)

            def carry_wait():
                nc.vector.memset(scrap[:], 0.0)

            def normed(src, dst, st, ag, ep, rs, done, g):
                for b in range(B):
                    nc.vector.bn_stats(stats[:, b], src[:, b]).then_inc(st, 1)
                dve.wait_ge(st, B * (g + 1))
                carry_wait()
                for b in range(B):
                    nc.vector.bn_aggr(mv[:, b], stats[:, b]).then_inc(ag, 1)
                dve.wait_ge(ag, B * (g + 1))
                nc.vector.tensor_scalar(rstd[:], mv[:, :, 1], EPS_LN, None, ALU.add).then_inc(ep, 1)
                dve.wait_ge(rs, g + 1)
                for b in range(B):
                    nc.vector.tensor_scalar(dst[:, b], src[:, b], mv[:, b, 0:1], rstd[:, b:b + 1], ALU.subtract, ALU.mult
                                            ).then_inc(done, 1)

            with dve.Fori(0, NCH) as g:
                dve.wait_ge(m_x, 16 * (g + 1))
                dve.wait_ge(m_seed, PRIMED + g)
                dve.wait_ge(acc_done, PRIMED + 2 * H * NCH)
                nc.vector.tensor_tensor(x1[:], xn[:], acc[:, g], ALU.add).then_inc(m_y, 1)
                dve.wait_ge(m_y, g + 1)
                normed(x1, x1, m_st, m_ag, m_ep, m_rs, m_x1, g)
                dve.wait_ge(m_lg, g + 1)
                nc.vector.tensor_tensor(logit, b4[:, 0:B * E].rearrange("p (b e) -> p b e", b=B),
                                        bcast(rbias[:].unsqueeze(1), [P, B, E]), ALU.add).then_inc(m_lb, 1)
                dve.wait_ge(m_lb, g + 1)
                nc.vector.reduce_max(nmax[:], logit, mybir.AxisListType.X).then_inc(m_mx, 1)
                dve.wait_ge(m_mx, g + 1)
                nc.vector.tensor_scalar(nmax[:], nmax[:], -1.0, None, ALU.mult).then_inc(m_nm, 1)
                dve.wait_ge(m_ex, B * (g + 1))
                nc.vector.reciprocal(den[:, 1], den[:, 0]).then_inc(m_rc, 1)
                dve.wait_ge(m_rc, g + 1)
                nc.vector.tensor_tensor(logit, logit, bcast(den[:, 1].unsqueeze(2), [P, B, E]), ALU.mult).then_inc(m_pr, 1)
                dve.wait_ge(m_pr, g + 1)
                carry_wait()
                for b in range(B):
                    nc.vector.max(top[:, b], logit[:, b]).then_inc(m_tp, 1)
                dve.wait_ge(m_tp, B * (g + 1))
                carry_wait()
                for b in range(B):
                    nc.vector.max_index(topi[:, b], top[:, b], logit[:, b]).then_inc(m_ti, 1)
                dve.wait_ge(m_ti, B * (g + 1))
                nc.vector.tensor_copy(topf, topi).then_inc(m_tf, 1)
                nc.vector.tensor_tensor(tsum[:], top[:, :, 0], top[:, :, 1], ALU.add).then_inc(m_ts, 1)
                dve.wait_ge(m_ts, g + 1)
                nc.vector.tensor_scalar(tsum[:], tsum[:], EPS_TOPK, None, ALU.add).then_inc(m_te, 1)
                dve.wait_ge(m_te, g + 1)
                nc.vector.reciprocal(tsum[:], tsum[:]).then_inc(m_tr2, 1)
                dve.wait_ge(m_tr2, g + 1)
                nc.vector.tensor_tensor(tw[:], top[:, :, 0:2], bcast(tsum[:].unsqueeze(2), [P, B, 2]), ALU.mult).then_inc(m_tw, 1)
                dve.wait_ge(m_tw, g + 1)
                dve.wait_ge(m_tf, g + 1)
                for x, s in ((0, m_s0), (1, m_s1)):
                    for b in range(B):
                        nc.vector.tensor_scalar(wsel[:, x, b], iot[:], topf[:, b, x:x + 1], tw[:, b, x:x + 1],
                                                ALU.is_equal, ALU.mult).then_inc(s, 1)
                dve.wait_ge(m_s0, B * (g + 1))
                dve.wait_ge(m_s1, B * (g + 1))
                nc.vector.tensor_tensor(wexp[:, 0:E].rearrange("p e b -> p b e"), wsel[:, 0], wsel[:, 1], ALU.add).then_inc(m_we, 1)
                dve.wait_ge(m_we, g + 1)

                n0 = g * (E + 1)
                dve.wait_ge(silu_e, n0 + 1)
                dve.wait_ge(ht_mm, PRIMED + n0)
                for b in range(B):
                    ins = nc.vector.scalar_tensor_tensor(hw[0][:, b], sg[0][:, b], wexp[:, 0, b:b + 1], gu[0][:, b, I:2 * I],
                                                         ALU.mult, ALU.mult)
                ins.then_inc(h_e, 1)
                with dve.Fori(0, E // 2) as e2:
                    for s in range(2):
                        n = n0 + e2 * 2 + s
                        dve.wait_ge(silu_e, n + 2)
                        dve.wait_ge(ht_mm, PRIMED + n)
                        for b in range(B):
                            ins = nc.vector.scalar_tensor_tensor(hw[1 - s][:, b], sg[1 - s][:, b],
                                                                 wexp[:, e2 * 2 + (s + 1), b:b + 1],
                                                                 gu[1 - s][:, b, I:2 * I], ALU.mult, ALU.mult)
                        ins.then_inc(h_e, 1)
                dve.wait_ge(m_fin, g + 1)
                dve.wait_ge(m_out, PRIMED + 16 * g)
                for half in range(2):
                    ins = nc.vector.tensor_copy(yo[:, 2 * half:2 * half + 2].rearrange("p b n -> p (b n)"), (b5, b6)[half][:])
                ins.then_inc(m_s2, 1)
                dve.wait_ge(m_s2, PRIMED + g + 1)
                normed(yo, yo, m_st2, m_ag2, m_ep2, m_rs2, m_yo, g)

        @block.tensor
        def _(pe):
            def mm(o, l, r, start=True, stop=True, **kw):
                return nc.tensor.matmul(o, l, r, start=start, stop=stop, **kw)

            pe.wait_ge(s_ld, 16 * 13)
            pe.wait_ge(s_const, 1)
            mm(b4[:, 0:H], onesrow, alog)
            for k in range(KT):
                ins = nc.tensor.transpose(b4[:, 64 + k * E:64 + (k + 1) * E], wrn[:, k * P:(k + 1) * P], ident[0:E, 0:E])
            ins.then_inc(s_apm, 1)
            bw = U[:, 0, 0:KT * H].rearrange("p (k h) -> p k h", k=KT)
            with pe.Fori(0, NCH) as c:
                pe.wait_ge(s_xin, 16 * (c + 1))
                pe.wait_ge(s_xcp, PRIMED + c)
                for k in range(KT):
                    for b in range(B):
                        ins = nc.tensor.transpose(pj[:, 0, k, b * P:(b + 1) * P], xnat[:, b, k * P:(k + 1) * P], ident[:])
                ins.then_inc(s_xtr, 1)
                pe.wait_ge(s_xcp, PRIMED + c + 1)
                pe.wait_ge(s_xfc, PRIMED + c)
                for bank, w in ((b5, 0), (b6, 2)):
                    for k in range(KT):
                        ins = mm(bank[:], R[:, w + k], xs[:, k * 512:(k + 1) * 512], start=(k == 0), stop=(k == KT - 1))
                ins.then_inc(s_xfm, 1)
                pe.wait_ge(s_bc, PRIMED + c)
                pe.wait_ge(s_xtc, c + 1)
                for b in range(B):
                    for k in range(KT):
                        ins = mm(b7[:, b * H:(b + 1) * H], xs[:, k * 512 + b * P:k * 512 + (b + 1) * P], bw[:, k],
                                 start=(k == 0), stop=(k == KT - 1))
                ins.then_inc(s_bm, 1)
            pe.wait_ge(s_bc, PRIMED + NCH)
            pe.wait_ge(s_chain["act"], 4)

            def proj(x, j, h, c, part_of=(0, 1)):
                pe.wait_ge(w_loaded[x], 16 * h + 16)
                if 0 not in part_of:
                    pass
                elif x == 0:
                    wait(pe, sums_read, j)
                elif x == 1:
                    pe.wait_ge(f_relu, j + 1)
                elif x == 2:
                    pe.wait_ge(conv_done[0], j + 1)
                for half in part_of:
                    for k in range(KT):
                        ins = mm(pair[x % 2][:, 2 * half:2 * half + 2, 0:W], wqkv[:, x, k], xT[:, k, c, 2 * half:2 * half + 2, :],
                                 start=(k == 0), stop=(k == KT - 1))
                if 1 in part_of:
                    ins.then_inc(proj_done[x], 1)

            def proj_f(j, h, c):
                pe.wait_ge(w_loaded[3], 16 * h + 16)
                wait(pe, gate_done, j)
                mm(bank_f, wf2[:], xf[:, c]).then_inc(proj_done[3], 1)

            def proj_g(j, h, c):
                pe.wait_ge(w_loaded[4], 16 * h + 16)
                pe.wait_ge(conv_done[1], j + 1)
                mm(bank_g, wg2[:], xg[:, c]).then_inc(proj_done[4], 1)

            def sums(j):
                pe.wait_ge(conv_done[2], j + 1)
                for x in range(2):
                    pe.wait_ge(sq_done[x], j + 1)
                    for b in range(B):
                        ins = mm(sums_qk[:, x, b:b + 1], sq[:, x, b], ones[:])
                ins.then_inc(sums_done, 1)

            def prologue(j, h, c):
                proj_f(j, h, c)
                proj(0, j, h, c)
                proj(1, j, h, c)
                proj(2, j, h, c)
                proj_g(j, h, c)
                sums(j)

            def body(i, h, c, hn, cn):
                j = i + 1

                def level(l):
                    n = 1 << l
                    if l == 0:
                        pe.wait_ge(init_done, i + 1)
                        pe.wait_ge(kr_init, i + 1)
                        pe.wait_ge(acc_done, PRIMED + 2 * i)
                    else:
                        pe.wait_ge(lvl_upd, upto(l - 1, i))
                        pe.wait_ge(qk_done, upto(l - 1, i))
                    right = FQ[:].rearrange("p x b (m two n) -> p x b m two n", two=2, n=n)[:, :, :, :, 1, :]
                    for b in range(B):
                        ins = mm(quad(b4)[:, b], KR[:, b], right[:, :, b])
                    ins.then_inc(lvl_mm, 1)

                def x_(l):
                    n = 1 << l
                    pe.wait_ge(kk_done, upto(l, i))
                    if l == 0:
                        pe.wait_ge(tt_init, i + 1)
                        pe.wait_ge(vp_done, i + 1)
                    else:
                        pe.wait_ge(t_add, i * (LEVELS - 1) + l)
                    left, _ = halves(TM[:], n)
                    for b in range(B):
                        ins = mm(part(b5, 0, n)[:, b], NT[:, l, b], left[:, b])
                    ins.then_inc(x_mm, 1)

                def t_(l):
                    n = 1 << l
                    pe.wait_ge(x_done, upto(l, i))
                    if l == 0:
                        pe.wait_ge(acc_done, PRIMED + 2 * i)
                    else:
                        pe.wait_ge(tt_add, upto(l - 1, i))
                    left, _ = halves(XL[:, l], n)
                    for b in range(B):
                        ins = mm(part(b6, 0, n)[:, b], TT[:, b], left[:, b])
                    ins.then_inc(t_mm, 1)

                def tt_(l):
                    n = 1 << l
                    pe.wait_ge(x_done, upto(l, i))
                    if l == 0:
                        pe.wait_ge(at_init, i + 1)
                    else:
                        pe.wait_ge(tt_add, upto(l - 1, i))
                    _, right = halves(TT[:], n)
                    for b in range(B):
                        ins = mm(part(b7, 0, n)[:, b], XL[:, l, b], right[:, b])
                    ins.then_inc(tt_mm, 1)

                pe.wait_ge(s_done, PRIMED + i)
                pe.wait_ge(silu_done[2], i + 1)
                for b in range(B):
                    ins = mm(quad(b7)[:, b], qkd[:, 1, b], qkd[:, 0, b])
                ins.then_inc(diag_done, 1)
                pe.wait_ge(r_ready, PRIMED + i)
                for b in range(B):
                    ins = nc.tensor.transpose(quad(b5)[:, b], qkd[:, 2, b], ident[:])
                ins.then_inc(vt_done, 1)
                level(0)
                proj_f(j, hn, cn)
                level(1)
                x_(0)
                proj(0, j, hn, cn, (0,))
                t_(0)
                level(2)
                tt_(0)
                x_(1)
                proj(0, j, hn, cn, (1,))
                t_(1)
                level(3)
                tt_(1)
                x_(2)
                proj(1, j, hn, cn, (0,))
                t_(2)
                level(4)
                tt_(2)
                x_(3)
                proj(1, j, hn, cn, (1,))
                t_(3)
                level(5)
                tt_(3)
                x_(4)
                proj(2, j, hn, cn, (0,))
                t_(4)
                level(6)
                tt_(4)
                x_(5)
                pe.wait_ge(lvl_upd, upto(6, i))
                pe.wait_ge(qk_done, upto(6, i))
                for b in range(B):
                    ins = nc.tensor.transpose(quad(b4)[:, b], KR[:, b], ident[:])
                ins.then_inc(krt_mm, 1)
                proj(2, j, hn, cn, (1,))
                t_(5)
                tt_(5)
                x_(6)
                pe.wait_ge(krt_done, i + 1)
                for b in range(B):
                    ins = mm(quad(b4)[:, b], FQ[:, 0, b], S[:, b])
                ins.then_inc(y_mm, 1)
                tt_(6)
                sums(j)
                pe.wait_ge(tt_add, upto(6, i))
                pe.wait_ge(r_done, i + 1)
                for b in range(B):
                    ins = mm(quad(b5)[:, b], TT[:, b], R[:, b])
                ins.then_inc(u_mm, 1)
                for b in range(B):
                    mm(quad(b6)[:, b], S[:, b], FQ[:, 1, b], start=(b == 0), stop=False, skip_group_check=True)
                proj_g(j, hn, cn)
                pe.wait_ge(u_done, i + 1)
                for b in range(B):
                    ins = mm(quad(b6)[:, b], U[:, b], AT[:, b], start=False, stop=(b == B - 1), skip_group_check=True)
                ins.then_inc(o_mm, 1)
                for b in range(B):
                    ins = mm(quad(b7)[:, b], KRt[:, b], U[:, b])
                ins.then_inc(s_mm, 1)
                pe.wait_ge(o2_done, PRIMED + i + 1)
                for b in range(B):
                    ins = mm(b5[:, b:b + 1], sq[:, 0, b], ones[:])
                ins.then_inc(osum_mm, 1)
                pe.wait_ge(g_done, i + 1)
                for b in range(B):
                    ins = mm((b4, b6)[b // 2][:, (b % 2) * D:(b % 2 + 1) * D], G[:, b], ow[:, h, :])
                ins.then_inc(out_mm, 1)

            over_quads(pe, prologue, body)

            pe.wait_ge(m_w, 16 * 10)
            with pe.Fori(0, NCH) as g:
                pe.wait_ge(m_x1, B * (g + 1))
                for k in range(KT):
                    for b in range(B):
                        ins = nc.tensor.transpose(pj[:, 0, k, b * P:(b + 1) * P], x1[:, b, k * P:(k + 1) * P], ident[:])
                ins.then_inc(m_tr, 1)
                pe.wait_ge(m_s2, PRIMED + g)
                for half in range(2):
                    ins = mm((b5, b6)[half][:], ident[:], x1[:, 2 * half:2 * half + 2].rearrange("p b n -> p (b n)"),
                             start=True, stop=False, skip_group_check=True)
                ins.then_inc(m_seed, 1)
                pe.wait_ge(m_xT, g + 1)
                pe.wait_ge(ht_e, PRIMED + (E + 1) * g)
                for b in range(B):
                    for k in range(KT):
                        ins = mm(b4[:, b * E:(b + 1) * E], x1T[:, k, b * P:(b + 1) * P], wrT[:, k], start=(k == 0), stop=(k == KT - 1))
                ins.then_inc(m_lg, 1)

                def transpose_h(s, n):
                    pe.wait_ge(h_e, PRIMED + n + 1)
                    pe.wait_ge(ht_e, PRIMED + n)
                    for b in range(B):
                        ins = nc.tensor.transpose(quad(b4)[:, b], hw[s][:, b], ident[:])
                    ins.then_inc(ht_mm, 1)

                def down(e, s, n, last, done):
                    pe.wait_ge(ht_e, PRIMED + n + 1)
                    for b in range(B):
                        ins = mm((b5, b6)[b // 2][:, (b % 2) * D:(b % 2 + 1) * D], hT[s][:, b], wdn[:, e, :],
                                 start=False, stop=last, skip_group_check=True)
                    ins.then_inc(done, 1)

                n0 = g * (E + 1)
                pe.wait_ge(m_lb, g + 1)
                pe.wait_ge(h_e, PRIMED + n0)
                for b in range(B):
                    for k in range(KT):
                        ins = mm(gu[0][:, b], x1T[:, k, b * P:(b + 1) * P], wgu[:, k, 0, :], start=(k == 0), stop=(k == KT - 1))
                ins.then_inc(gu_mm, 1)
                with pe.Fori(0, E // 2) as e2:
                    for s in range(2):
                        n = n0 + e2 * 2 + s
                        pe.wait_ge(h_e, PRIMED + n)
                        for b in range(B):
                            for k in range(KT):
                                ins = mm(gu[1 - s][:, b], x1T[:, k, b * P:(b + 1) * P], wgu[:, k, e2 * 2 + (s + 1), :],
                                         start=(k == 0), stop=(k == KT - 1))
                        ins.then_inc(gu_mm, 1)
                        transpose_h(s, n)
                        down(e2 * 2 + s, s, n, False, dn_mm)
                transpose_h(0, n0 + E)
                down(E, 0, n0 + E, True, m_fin)


NAMES = {"x": "L0_attn_hidden_states"}
NAMES.update({n: "L0_attn_" + n for n in (
    "q_w", "k_w", "v_w", "q_conv_w", "k_conv_w", "v_conv_w", "f_w1", "f_w2", "b_w", "A_log", "dt_bias",
    "g_w1", "g_w2", "g_b2", "o_norm_w", "o_w")})
NAMES.update({n: "L0_ffn_" + n for n in ("Wr", "bias", "Wg", "Wu", "Wd", "sWg", "sWu", "sWd")})


def kernel(**inputs):
    import concourse.bacc as bacc
    from concourse.bass_utils import run_bass_kernel_spmd

    nc = bacc.Bacc("TRN2", target_bir_lowering=False, num_devices=1)
    arrays, aps = {}, {}
    for short, name in NAMES.items():
        v = np.ascontiguousarray(inputs[name])
        arrays[f"in_{name}"] = v
        aps[short] = nc.dram_tensor(f"in_{name}", v.shape, mybir.dt.from_np(v.dtype), kind="ExternalInput").ap()
    out = nc.dram_tensor("out", (B, T, D), FP, kind="ExternalOutput").ap()
    build(nc, aps, out)
    r = run_bass_kernel_spmd(nc, [arrays], core_ids=[0])
    return r.results[0]["out"]
```

```python
from contextlib import ExitStack

import numpy as np

import concourse.bass as bass
from concourse import mybir

FP = mybir.dt.float32
U32 = mybir.dt.uint32
ALU = mybir.AluOpType
ACT = mybir.ActivationFunctionType

B, T, D = 4, 1024, 256
H, DK = 16, 128
P = 128
KT = D // P
NCH = T // P
TAPS = 4
HALO = TAPS - 1
W = P + HALO
LEVELS = 7
HALF = P // 2
PRIMED = 1
E = 16
I = 128
EPS_NORM, EPS_L2, EPS_TOPK, EPS_LN = 1e-5, 1e-6, 1e-9, 1e-5


def build(nc, a, out):
    ctx = ExitStack()
    with ctx:
        def sb(name, shape, dt=FP):
            return ctx.enter_context(nc.sbuf_tensor(name, shape, dt))

        def ps(name):
            return ctx.enter_context(nc.psum_tensor(name, [P, 512], FP))

        def sem(name):
            return ctx.enter_context(nc.semaphore(name))

        def sems(name, n):
            return [sem(f"{name}{k}") for k in range(n)]

        XT = KT * (NCH + 1) * B * W
        XF = NCH * B * P
        arena = sb("arena", [P, XT + 2 * XF])
        xT = arena[:, 0:XT].rearrange("p (k c b w) -> p k c b w", k=KT, c=NCH + 1, b=B)
        xf = arena[:, XT:XT + XF].rearrange("p (c n) -> p c n", c=NCH)
        xg = arena[:, XT + XF:XT + 2 * XF].rearrange("p (c n) -> p c n", c=NCH)
        wgu = arena[:, 0:KT * (E + 1) * 2 * I].rearrange("p (k e n) -> p k e n", k=KT, e=E + 1)
        wdn = arena[:, KT * (E + 1) * 2 * I:(KT * 2 * I + D) * (E + 1)].rearrange("p (e n) -> p e n", e=E + 1)
        acc = sb("acc", [P, NCH, B, D])
        ow = sb("ow", [P, H, D])
        wqkv = sb("wqkv", [P, 3, KT, DK])
        wf2 = sb("wf2", [P, DK])
        wg2 = sb("wg2", [P, DK])
        convw = sb("convw", [P, 3, H + 1, TAPS])
        dtb = sb("dtb", [P, H + 1])
        gb2h = sb("gb2h", [P, H + 1])
        negA = sb("negA", [P, H + 1])
        beta = sb("beta", [P, H + 1, NCH, B])
        onw = sb("onw", [P, 1])
        ident = sb("ident", [P, P])
        ones = sb("ones", [P, 1])
        keep = sb("keep", [P, NCH])
        mhalf = sb("mhalf", [P, 16])
        mask = sb("mask", [P, LEVELS, HALF])
        qkd = sb("qkd", [P, 4, B, P])
        pre = sb("pre", [P, 2, B, P])
        sq = sb("sq", [P, 2, B, P])
        fsp = sb("fsp", [P, 4, B, P])
        FQ = sb("FQ", [P, 2, B, P])
        KR = sb("KR", [P, B, P])
        PB = sb("PB", [P, B * (P - 1)])
        NT = sb("NT", [P, LEVELS, B, P])
        XL = sb("XL", [P, LEVELS, B, P])
        TM = sb("TM", [P, B, P])
        TT = sb("TT", [P, B, P])
        AT = sb("AT", [P, B, P])
        R = sb("R", [P, B, P])
        U = sb("U", [P, B, P])
        KRt = sb("KRt", [P, B, P])
        S = sb("S", [P, B, P])
        gt = sb("gt", [P, B, P])
        G = sb("G", [P, B, P])
        onesrow, alog = KRt[0:1, 0], KRt[0:1, 1, 0:H]
        nxt = sb("nxt", [P, 4, B])
        cur = sb("cur", [P, 4, B])
        qk = sb("qk", [P, B])
        ssum = sb("ssum", [P, 2, B])
        sinv = sb("sinv", [P, 2, B])
        rr = sb("rr", [P, 3, B])
        flatN = NT[:].rearrange("p l b n -> p (l b n)")
        flatZ = XL[:].rearrange("p l b n -> p (l b n)")
        xn = flatN[:, 0:1024].rearrange("p (b n) -> p b n", b=B)
        x1 = flatN[:, 1024:2048].rearrange("p (b n) -> p b n", b=B)
        x1T = flatN[:, 2048:3072].rearrange("p (k n) -> p k n", k=KT)
        yo = flatZ[:, 0:1024].rearrange("p (b n) -> p b n", b=B)
        sg = [flatZ[:, 1024 + 512 * s:1536 + 512 * s].rearrange("p (b n) -> p b n", b=B) for s in range(2)]
        hw = [qkd[:, s] for s in range(2)]
        hT = [qkd[:, 2 + s] for s in range(2)]
        scrap = sb("scrap", [P, 1])
        stats = sb("stats", [P, B, 6])
        mv = sb("mv", [P, B, 2])
        rstd = sb("rstd", [P, B])
        wrn = G[0:E, 0:2].rearrange("p a n -> p (a n)")
        wrT = sb("wrT", [P, KT, E])
        rbias = sb("rbias", [P, E])
        logit = AT[:, 0, 0:B * E].rearrange("p (b e) -> p b e", b=B)
        nmax = sb("nmax", [P, B])
        den = sb("den", [P, 2, B])
        top, topi, topf = (AT[:, 2, 8 * B * x:8 * B * (x + 1)].rearrange("p (b n) -> p b n", b=B) for x in range(3))
        topi = topi.bitcast(U32)
        tsum = sb("tsum", [P, B])
        tw = sb("tw", [P, B, 2])
        iot = sb("iot", [P, E])
        wsel = AT[:, 1, 0:2 * B * E].rearrange("p (x b e) -> p x b e", x=2, b=B)
        wexp = sb("wexp", [P, E + 1, B])

        pj = ctx.enter_context(nc.psum_tensor("pj", [P, 2, 2, 512], FP))
        b4, b5, b6, b7 = ps("b4"), ps("b5"), ps("b6"), ps("b7")
        pair = [pj[:, n].rearrange("p a (x w) -> p (a x) w", x=2) for n in range(2)]
        xnat = pre[:].rearrange("p a b n -> p (a b n)").rearrange("p (b n) -> p b n", b=B)
        xs = fsp[:, 0:2].rearrange("p a b n -> p (a b n)")
        gu = pair
        bank_f, bank_g = pj[:, 1, 0], pj[:, 1, 1]
        sums_qk = bank_f[:, 0:3 * B].rearrange("p (x b) -> p x b", x=3)
        sums_o = bank_f[:, 3 * B:4 * B]

        def quad(bank):
            return bank[:, 0:512].rearrange("p (b n) -> p b n", b=B)

        def halves(ap, n):
            v = ap.rearrange("p b (m two n) -> p b m two n", two=2, n=n)
            return v[:, :, :, 0, :], v[:, :, :, 1, :]

        def part(bank, lo, n):
            return bank[:, lo:lo + B * HALF].rearrange("p (b m n) -> p b m n", b=B, n=n)

        s_const = sem("s_const")
        s_chain = {k: sem(f"s_chain_{k}") for k in ("pool", "dve", "act")}
        s_ld = sem("s_ld")
        s_xin, s_xtr, s_xcp, s_xtc, s_xfm, s_xfc = (sem(n) for n in ("s_xin", "s_xtr", "s_xcp", "s_xtc", "s_xfm", "s_xfc"))
        s_bm, s_bc, s_apm = sem("s_bm"), sem("s_bc"), sem("s_apm")
        w_loaded = sems("w_loaded", 5)
        proj_done = sems("proj_done", 5)
        tap_done = sems("tap_done", 3)
        conv_step = sems("conv_step", 3)
        conv_done = sems("conv_done", 3)
        silu_done = sems("silu_done", 3)
        sq_done = sems("sq_done", 2)
        qk_prod = sem("qk_prod")
        sums_done, sums_read, inv_done, nxt1, nxt_done, cur_done = (
            sem(n) for n in ("sums_done", "sums_read", "inv_done", "nxt1", "nxt_done", "cur_done"))
        cur_beta = sem("cur_beta")
        f_abs, f_relu, f_exp, f_ln, f_w1, f_sub, f_add, f_sum, d_exp, d_done, gate_done = (
            sem(n) for n in ("f_abs", "f_relu", "f_exp", "f_ln", "f_w1", "f_sub", "f_add", "f_sum", "d_exp", "d_done", "gate_done"))
        init_done, tm_init, tt_init, vt_done, at_init, vp_done = (
            sem(n) for n in ("init_done", "tm_init", "tt_init", "vt_done", "at_init", "vp_done"))
        x_mm, x_done, t_mm, t_add, kr_init = (sem(n) for n in ("x_mm", "x_done", "t_mm", "t_add", "kr_init"))
        lvl_mm = sem("lvl_mm")
        blk_done = sem("blk_done")
        lvl_upd = sem("lvl_upd")
        kk_done = sem("kk_done")
        qk_done = sem("qk_done")
        tt_mm = sem("tt_mm")
        tt_copied = sem("tt_copied")
        krt_mm, krt_done, y_mm, r_done, u_mm, u_done, o_mm, s_mm, s_done = (
            sem(n) for n in ("krt_mm", "krt_done", "y_mm", "r_done", "u_mm", "u_done", "o_mm", "s_mm", "s_done"))
        g_done, o2_done, osum_mm, ms_done, ms_eps, ms_pow, r_ready, out_mm, acc_done = (
            sem(n) for n in ("g_done", "o2_done", "osum_mm", "ms_done", "ms_eps", "ms_pow", "r_ready", "out_mm", "acc_done"))
        m_w = sem("m_w")
        (m_x, m_y, m_st, m_ag, m_ep, m_rs, m_x1, m_tr, m_xT, m_lg, m_lb, m_mx, m_nm, m_ex, m_de, m_rc, m_pr, m_tp, m_ti, m_tf,
         m_ts, m_te, m_tr2, m_tw, m_s0, m_s1, m_we, m_seed, m_fin, m_s2, m_st2, m_ag2, m_ep2, m_rs2, m_yo, m_out) = (
            sem(n) for n in ("m_x m_y m_st m_ag m_ep m_rs m_x1 m_tr m_xT m_lg m_lb m_mx m_nm m_ex m_de m_rc m_pr m_tp m_ti m_tf "
                             "m_ts m_te m_tr2 m_tw m_s0 m_s1 m_we m_seed m_fin m_s2 m_st2 m_ag2 m_ep2 m_rs2 m_yo m_out").split())
        gu_mm, silu_e, h_e, ht_mm, ht_e, dn_mm = (sem(n) for n in ("gu_mm", "silu_e", "h_e", "ht_mm", "ht_e", "dn_mm"))

        def wait(eng, s, value):
            if isinstance(value, int) and value <= 0:
                return
            eng.wait_ge(s, value)

        def upto(l, i, levels=LEVELS):
            return i * levels + (l + 1)

        def over_quads(eng, stage_a, body):
            stage_a(0, 0, 0)
            with eng.Fori(0, H) as h:
                with eng.Fori(0, NCH - 1) as c:
                    body(h * NCH + c, h, c, h, c + 1)
                body(h * NCH + (NCH - 1), h, NCH - 1, h + 1, 0)

        def bcast(ap, shape):
            return ap.to_broadcast(shape)

        block = ctx.enter_context(nc.Block())
        names = ("q", "k", "v")

        @block.sync
        def _(sp):
            for s in (o_mm, r_ready, acc_done, s_done, o2_done, osum_mm, ms_done, s_bm, s_xcp, s_xfc, s_bc, m_seed, m_s2, m_out,
                      h_e, ht_e, ht_mm):
                sp.sem_inc(s, PRIMED)
            n = 0
            for dst, src in (
                (convw[:, 0, 0:H], a["q_conv_w"].rearrange("(h p) t -> p h t", p=P)),
                (convw[:, 1, 0:H], a["k_conv_w"].rearrange("(h p) t -> p h t", p=P)),
                (convw[:, 2, 0:H], a["v_conv_w"].rearrange("(h p) t -> p h t", p=P)),
                (dtb[:, 0:H], a["dt_bias"].rearrange("(h p) -> p h", p=P)),
                (gb2h[:, 0:H], a["g_b2"].rearrange("(h p) -> p h", p=P)),
                (alog, a["A_log"].rearrange("(o h) -> o h", o=1)),
                (onw[:], a["o_norm_w"].rearrange("(p o) -> p o", o=1)),
                (ow[:], a["o_w"].rearrange("(h p) n -> p h n", p=P)),
                (wrn, a["Wr"]),
                (R[:, 0:2], a["f_w1"].rearrange("(k p) n -> p k n", p=P)),
                (R[:, 2:4], a["g_w1"].rearrange("(k p) n -> p k n", p=P)),
                (U[:, 0, 0:KT * H].rearrange("p (k h) -> p k h", k=KT), a["b_w"].rearrange("(k p) n -> p k n", p=P)),
                (rbias[:], a["bias"].partition_broadcast(P)),
            ):
                sp.dma_start(dst, src, allow_slow_non_contiguous=True).then_inc(s_ld, 16)
                n += 1

            def weights(h, prev):
                for x, name in enumerate(("q_w", "k_w", "v_w")):
                    wait(sp, proj_done[x], prev)
                    sp.dma_start(wqkv[:, x], a[name].rearrange("(k p) (h n) -> p k h n", p=P, n=DK)[:, :, h, :]
                                 ).then_inc(w_loaded[x], 16)
                for x, (dst, name) in enumerate(((wf2, "f_w2"), (wg2, "g_w2"))):
                    wait(sp, proj_done[3 + x], prev)
                    sp.dma_start(dst[:], a[name].rearrange("p (h n) -> p h n", n=DK)[:, h, :]).then_inc(w_loaded[3 + x], 16)

            xsrc = a["x"].rearrange("b (c p) d -> p c b d", p=P)
            sp.dma_start(xnat, xsrc[:, 0]).then_inc(s_xin, 16)
            weights(0, 0)
            with sp.Fori(1, NCH) as c:
                sp.wait_ge(s_xtr, c)
                sp.dma_start(xnat, xsrc[:, c]).then_inc(s_xin, 16)
            with sp.Fori(1, H) as h:
                weights(h, h * NCH)
            weights(0, H * NCH)

            sp.wait_ge(proj_done[4], H * NCH + 1)
            for k in range(KT):
                for x, (name, shared) in enumerate((("Wg", "sWg"), ("Wu", "sWu"))):
                    sp.dma_start(wgu[:, k, 0:E, x * I:(x + 1) * I],
                                 a[name].rearrange("e (k p) n -> p k e n", p=P)[:, k]).then_inc(m_w, 16)
                    sp.dma_start(wgu[:, k, E, x * I:(x + 1) * I],
                                 a[shared].rearrange("(k p) n -> p k n", p=P)[:, k]).then_inc(m_w, 16)
            sp.dma_start(wdn[:, 0:E], a["Wd"].rearrange("e p n -> p e n")).then_inc(m_w, 16)
            sp.dma_start(wdn[:, E], a["sWd"]).then_inc(m_w, 16)
            sp.wait_ge(out_mm, H * NCH)
            odst = out.rearrange("b (c p) d -> p c b d", p=P)
            sp.dma_start(xn, xsrc[:, 0]).then_inc(m_x, 16)

            def store(g):
                sp.wait_ge(m_yo, (g + 1) * B)
                sp.dma_start(odst[:, g], yo).then_inc(m_out, 16)

            with sp.Fori(0, NCH - 1) as g:
                sp.wait_ge(m_y, g + 1)
                sp.dma_start(xn, xsrc[:, g + 1]).then_inc(m_x, 16)
                store(g)
            store(NCH - 1)
            sp.wait_ge(m_out, PRIMED + 16 * NCH)

        @block.gpsimd
        def _(pool):
            cnt = [0]

            def link(ins):
                cnt[0] += 1
                ins.then_inc(s_chain["pool"], 1)
                pool.wait_ge(s_chain["pool"], cnt[0])

            for t, v in ((ident[:], 0.0), (ones[:], 1.0), (onesrow, 1.0), (keep[:], 1.0), (mhalf[:], -0.5),
                         (mask[:], 1.0), (NT[:], 0.0), (XL[:], 0.0), (S[:], 0.0),
                         (xT[:, :, 0, :, 0:HALO], 0.0), (convw[:, :, H], 0.0), (dtb[:, H:H + 1], 0.0),
                         (gb2h[:, H:H + 1], 0.0), (negA[:, H:H + 1], 0.0), (beta[:, H], 0.0), (wexp[:, E], 1.0)):
                link(nc.gpsimd.memset(t, v))
            link(nc.gpsimd.memset(keep[:, 0:1], 0.0))
            link(nc.gpsimd.iota(topi[:, 0:2, :].rearrange("p b n -> p (b n)").bitcast(mybir.dt.int32), [[1, E]], base=0, channel_multiplier=0))
            link(nc.gpsimd.tensor_copy(iot[:], topi[:, 0:2, :].rearrange("p b n -> p (b n)").bitcast(mybir.dt.int32)))
            link(nc.gpsimd.affine_select(out=ident[:], in_=ident[:], compare_op=ALU.not_equal, fill=1.0, base=0,
                                         pattern=[[-1, P]], channel_multiplier=1))
            for l in range(LEVELS):
                n = 1 << l
                m = HALF // n
                v = mask[:, l].rearrange("p (m n) -> p m n", n=n)
                link(nc.gpsimd.affine_select(out=v, in_=v, compare_op=ALU.is_ge, fill=0.0, base=0,
                                             pattern=[[-2 * n, m], [0, n]], channel_multiplier=1))
                link(nc.gpsimd.affine_select(out=v, in_=v, compare_op=ALU.is_ge, fill=0.0, base=n - 1,
                                             pattern=[[2 * n, m], [0, n]], channel_multiplier=-1))
            nc.gpsimd.memset(acc[:], 0.0).then_inc(s_const, 1)

            def softplus_add(j):
                pool.wait_ge(f_relu, j + 1)
                pool.wait_ge(f_sub, j + 1)
                nc.gpsimd.tensor_tensor(fsp[:, 3], fsp[:, 3], fsp[:, 0], ALU.add).then_inc(f_add, 1)

            def softplus_sum(j):
                pool.wait_ge(f_add, j + 1)
                pool.wait_ge(f_ln, j + 1)
                nc.gpsimd.tensor_tensor(fsp[:, 3], fsp[:, 3], fsp[:, 2], ALU.add).then_inc(f_sum, 1)

            def stage_a_prod(j):
                pool.wait_ge(silu_done[1], j + 1)
                nc.gpsimd.tensor_tensor(fsp[:, 2], qkd[:, 0], qkd[:, 1], ALU.mult).then_inc(qk_prod, 1)

            def stage_a_cols(j, h, c):
                pool.wait_ge(sums_read, j + 1)
                nc.gpsimd.tensor_tensor(sinv[:], ssum[:], mhalf[:, 0:2 * B].rearrange("p (x b) -> p x b", x=2), ALU.pow
                                        ).then_inc(inv_done, 1)
                pool.wait_ge(inv_done, j + 1)
                wait(pool, cur_done, j)
                nc.gpsimd.tensor_tensor(nxt[:, 0], sinv[:, 1], beta[:, h, c, :], ALU.mult).then_inc(nxt1, 1)
                nc.gpsimd.tensor_tensor(nxt[:, 3], sinv[:, 0], sinv[:, 0], ALU.mult)
                nc.gpsimd.tensor_copy(nxt[:, 2], sinv[:, 0])
                pool.wait_ge(nxt1, j + 1)
                nc.gpsimd.tensor_tensor(nxt[:, 1], nxt[:, 0], sinv[:, 1], ALU.mult).then_inc(nxt_done, 1)

            def stage_a_keep(j, h, c):
                pool.wait_ge(d_exp, j + 1)
                nc.gpsimd.tensor_tensor(qkd[:, 3, :, 0], qkd[:, 3, :, 0], bcast(keep[:, bass.ds(c, 1)], [P, B]), ALU.mult
                                        ).then_inc(d_done, 1)

            def init(j):
                pool.wait_ge(silu_done[1], j + 1)
                pool.wait_ge(d_done, j + 1)
                pool.wait_ge(o_mm, PRIMED + j)
                nc.gpsimd.tensor_tensor(FQ[:, 0], qkd[:, 1], qkd[:, 3], ALU.mult)
                nc.gpsimd.tensor_tensor(FQ[:, 1], qkd[:, 0], qkd[:, 3], ALU.mult).then_inc(init_done, 1)

            def prologue(j, h, c):
                pool.wait_ge(s_bc, PRIMED + NCH)
                softplus_add(j)
                softplus_sum(j)
                stage_a_keep(j, h, c)
                stage_a_prod(j)
                stage_a_cols(j, h, c)
                init(j)

            off = [0]
            for l in range(LEVELS):
                off.append(off[-1] + B * (HALF >> l))

            def blocks(l):
                if l == 0:
                    return qkd[:, 3].rearrange("p b n -> p (b n)")
                return PB[:, off[l - 1]:off[l]]

            def body(i, h, c, hn, cn):
                for l in range(LEVELS):
                    n = 1 << l
                    pl = blocks(l).rearrange("p (m two) -> p m two", two=2)
                    if l:
                        pool.wait_ge(blk_done, upto(l - 1, i))
                    nc.gpsimd.tensor_tensor(blocks(l + 1), pl[:, :, 0], pl[:, :, 1], ALU.mult).then_inc(blk_done, 1)
                    pool.wait_ge(lvl_mm, upto(l, i))
                    if l == 0:
                        pool.wait_ge(init_done, i + 1)
                    else:
                        pool.wait_ge(lvl_upd, upto(l - 1, i))
                    kl, _ = halves(KR[:], n)
                    kl = kl.rearrange("p b m n -> p (b m) n")
                    nc.gpsimd.tensor_tensor(kl, kl, bcast(pl[:, :, 1:2], [P, B * HALF // n, n]), ALU.mult)
                    fr = FQ[:].rearrange("p x b (m two n) -> p x (b m) two n", two=2, n=n)[:, :, :, 1, :]
                    nc.gpsimd.tensor_tensor(fr, fr, bcast(pl[:, :, 0:1].unsqueeze(1), [P, 2, B * HALF // n, n]), ALU.mult
                                            ).then_inc(lvl_upd, 1)
                    if l == 2:
                        softplus_add(i + 1)
                    if l == 3:
                        softplus_sum(i + 1)
                    if l == 5:
                        stage_a_keep(i + 1, hn, cn)
                stage_a_prod(i + 1)
                stage_a_cols(i + 1, hn, cn)
                init(i + 1)
                pool.wait_ge(ms_eps, i + 1)
                nc.gpsimd.tensor_tensor(rr[:, 1], rr[:, 0], mhalf[:, 0:B], ALU.pow).then_inc(ms_pow, 1)
                pool.wait_ge(ms_pow, i + 1)
                nc.gpsimd.tensor_tensor(rr[:, 2], rr[:, 1], cur[:, 2], ALU.mult).then_inc(r_ready, 1)

            over_quads(pool, prologue, body)

            with pool.Fori(0, NCH) as g:
                pool.wait_ge(m_ep, g + 1)
                nc.gpsimd.tensor_tensor(rstd[:], rstd[:], mhalf[:, 0:B], ALU.pow).then_inc(m_rs, 1)
                pool.wait_ge(m_ep2, g + 1)
                nc.gpsimd.tensor_tensor(rstd[:], rstd[:], mhalf[:, 0:B], ALU.pow).then_inc(m_rs2, 1)

        @block.scalar
        def _(act):
            act.wait_ge(s_ld, 16 * 13)
            act.wait_ge(s_const, 1)
            nc.scalar.mul(gb2h[:, 0:H], gb2h[:, 0:H], 0.5)
            act.wait_ge(s_apm, 1)
            nc.scalar.activation(negA[:, 0:H], b4[:, 0:H], ACT.Exp).then_inc(s_chain["act"], 1)
            act.wait_ge(s_chain["act"], 1)
            nc.scalar.mul(negA[:, 0:H], negA[:, 0:H], -1.0).then_inc(s_chain["act"], 1)
            nc.scalar.copy(wrT[:], b4[:, 64:64 + KT * E].rearrange("p (k e) -> p k e", k=KT)).then_inc(s_chain["act"], 1)
            nc.scalar.mul(ow[:], ow[:], onw[:]).then_inc(s_chain["act"], 1)
            act.wait_ge(s_chain["act"], 4)

            with act.Fori(0, NCH) as c:
                act.wait_ge(s_xtr, c + 1)
                act.wait_ge(s_bm, PRIMED + c)
                nc.scalar.copy(xs, pj[:, 0].rearrange("p a n -> p (a n)")).then_inc(s_xcp, 1)
                act.wait_ge(s_xfm, c + 1)
                nc.scalar.copy(xf[:, c], b5[:])
                nc.scalar.copy(xg[:, c], b6[:]).then_inc(s_xfc, 1)
                act.wait_ge(s_bm, PRIMED + c + 1)
                nc.scalar.activation(beta[:, 0:H, c, :].rearrange("p h b -> p b h"),
                                     b7[:, 0:B * H].rearrange("p (b h) -> p b h", b=B), ACT.Sigmoid).then_inc(s_bc, 1)

            def tap(x, j, h):
                act.wait_ge(proj_done[x], j + 1)
                if x == 2:
                    act.wait_ge(silu_done[0], j + 1)
                elif x == 0:
                    wait(act, silu_done[2], j)
                else:
                    wait(act, silu_done[1], j)
                nc.scalar.activation(pre[:, x % 2], pair[x % 2][:, :, 0:P], ACT.Copy, scale=convw[:, x, h, 0:1]
                                     ).then_inc(tap_done[x], 1)

            def silu(x, j):
                act.wait_ge(conv_done[x], j + 1)
                wait(act, init_done, j)
                wait(act, vt_done, j)
                wait(act, qk_prod, j)
                nc.scalar.activation(qkd[:, x], pre[:, x % 2], ACT.Silu).then_inc(silu_done[x], 1)

            def square(x, j):
                act.wait_ge(silu_done[x], j + 1)
                wait(act, sums_done, j)
                if x == 0:
                    wait(act, osum_mm, PRIMED + j - 1)
                nc.scalar.activation(sq[:, x], qkd[:, x], ACT.Square).then_inc(sq_done[x], 1)

            def f_start(j, h):
                act.wait_ge(proj_done[3], j + 1)
                wait(act, f_sum, j)
                f = quad(bank_f)
                nc.scalar.activation(fsp[:, 1], f, ACT.Abs, bias=dtb[:, bass.ds(h, 1)]).then_inc(f_abs, 1)
                nc.scalar.activation(fsp[:, 0], f, ACT.Relu, bias=dtb[:, bass.ds(h, 1)]).then_inc(f_relu, 1)

            def f_e(j):
                act.wait_ge(f_abs, j + 1)
                nc.scalar.activation(fsp[:, 1], fsp[:, 1], ACT.Exp, scale=-1.0).then_inc(f_exp, 1)

            def f_l(j):
                act.wait_ge(f_exp, j + 1)
                wait(act, sums_done, j)
                nc.scalar.activation(fsp[:, 2], fsp[:, 1], ACT.Ln, bias=1.0).then_inc(f_ln, 1)

            def f_d(j, h):
                act.wait_ge(f_sum, j + 1)
                wait(act, lvl_upd, upto(0, j - 1))
                wait(act, blk_done, upto(0, j - 1))
                nc.scalar.activation(qkd[:, 3], fsp[:, 3], ACT.Exp, scale=negA[:, bass.ds(h, 1)]).then_inc(d_exp, 1)

            def gate(j, h):
                act.wait_ge(proj_done[4], j + 1)
                wait(act, g_done, j)
                nc.scalar.activation(gt[:], quad(bank_g), ACT.Tanh, bias=gb2h[:, bass.ds(h, 1)], scale=0.5).then_inc(gate_done, 1)

            def prologue(j, h, c):
                f_start(j, h)
                f_e(j)
                f_l(j)
                tap(0, j, h)
                f_d(j, h)
                tap(1, j, h)
                silu(0, j)
                square(0, j)
                tap(2, j, h)
                silu(1, j)
                square(1, j)
                silu(2, j)
                gate(j, h)

            def body(i, h, c, hn, cn):
                j = i + 1

                f_start(j, hn)
                f_e(j)
                f_l(j)
                tap(0, j, hn)
                f_d(j, hn)
                tap(1, j, hn)
                silu(0, j)
                square(0, j)
                silu(1, j)
                square(1, j)
                tap(2, j, hn)
                act.wait_ge(krt_mm, i + 1)
                nc.scalar.copy(KRt[:], quad(b4)).then_inc(krt_done, 1)
                act.wait_ge(u_mm, i + 1)
                nc.scalar.copy(U[:], quad(b5)).then_inc(u_done, 1)
                silu(2, j)
                act.wait_ge(o_mm, PRIMED + i + 1)
                act.wait_ge(sums_done, j + 1)
                nc.scalar.activation(sq[:, 0], quad(b6), ACT.Square).then_inc(o2_done, 1)
                gate(j, hn)

            over_quads(act, prologue, body)

            with act.Fori(0, NCH) as g:
                act.wait_ge(m_tr, g + 1)
                nc.scalar.copy(x1T, pj[:, 0].rearrange("p a n -> p (a n)").rearrange("p (k n) -> p k n", k=KT)).then_inc(m_xT, 1)
                act.wait_ge(m_nm, g + 1)
                for b in range(B):
                    nc.scalar.activation(logit[:, b], logit[:, b], ACT.Exp, bias=nmax[:, b:b + 1],
                                         accum_out=den[:, 0, b:b + 1]).then_inc(m_ex, 1)

                n0 = g * (E + 1)
                act.wait_ge(gu_mm, n0 + 1)
                act.wait_ge(h_e, PRIMED + n0)
                nc.scalar.activation(sg[0], gu[0][:, :, 0:I], ACT.Silu).then_inc(silu_e, 1)
                with act.Fori(0, E // 2) as e2:
                    for s in range(2):
                        n = n0 + e2 * 2 + s
                        act.wait_ge(gu_mm, n + 2)
                        act.wait_ge(h_e, PRIMED + n)
                        nc.scalar.activation(sg[1 - s], gu[1 - s][:, :, 0:I], ACT.Silu).then_inc(silu_e, 1)
                        act.wait_ge(ht_mm, PRIMED + n + 1)
                        nc.scalar.copy(hT[s], quad(b4)).then_inc(ht_e, 1)
                act.wait_ge(ht_mm, PRIMED + n0 + E + 1)
                nc.scalar.copy(hT[0], quad(b4)).then_inc(ht_e, 1)

        @block.vector
        def _(dve):
            with dve.Fori(0, NCH) as c:
                dve.wait_ge(s_xcp, PRIMED + c + 1)
                v = xs.rearrange("p (k b n) -> p k b n", k=KT, b=B)
                for k in range(KT):
                    nc.vector.tensor_copy(xT[:, k, c, :, HALO:W], v[:, k])
                    ins = nc.vector.tensor_copy(xT[:, k, c + 1, :, 0:HALO], v[:, k, :, P - HALO:P])
                ins.then_inc(s_xtc, 1)

            def conv(x, j, h, taps=range(1, TAPS)):
                src = pair[x % 2]
                for t in taps:
                    if t == 1:
                        dve.wait_ge(tap_done[x], j + 1)
                    else:
                        dve.wait_ge(conv_step[x], 2 * j + t - 1)
                    nc.vector.scalar_tensor_tensor(
                        pre[:, x % 2], src[:, :, t:t + P], convw[:, x, h, t:t + 1], pre[:, x % 2], ALU.mult, ALU.add
                    ).then_inc(conv_done[x] if t == HALO else conv_step[x], 1)

            def f_low(j):
                dve.wait_ge(f_exp, j + 1)
                wait(dve, d_exp, j)
                nc.vector.tensor_scalar(fsp[:, 3], fsp[:, 1], 1.0, 1.0, ALU.add, ALU.subtract).then_inc(f_w1, 1)
                dve.wait_ge(f_w1, j + 1)
                nc.vector.tensor_tensor(fsp[:, 3], fsp[:, 1], fsp[:, 3], ALU.subtract).then_inc(f_sub, 1)

            def sums(j):
                dve.wait_ge(sums_done, j + 1)
                wait(dve, nxt_done, j)
                nc.vector.tensor_copy(qk[:], sums_qk[:, 2])
                nc.vector.tensor_scalar(ssum[:, 1], sums_qk[:, 1], EPS_L2, None, ALU.add)
                nc.vector.tensor_scalar(ssum[:, 0], sums_qk[:, 0], EPS_L2, float(DK), ALU.add, ALU.mult).then_inc(sums_read, 1)

            def prologue(j, h, c):
                f_low(j)
                conv(0, j, h)
                conv(1, j, h)
                conv(2, j, h)
                sums(j)
                init_k(j)
                init_t(j)
                init_cols(j)
                init_rest(j)

            def init_k(j):
                dve.wait_ge(silu_done[1], j + 1)
                wait(dve, krt_mm, j)
                nc.vector.tensor_copy(KR[:], qkd[:, 1]).then_inc(kr_init, 1)
                nc.vector.tensor_copy(TM[:], bcast(ident[:].unsqueeze(1), [P, B, P])).then_inc(tm_init, 1)

            def init_t(j):
                wait(dve, u_mm, j)
                nc.vector.tensor_copy(TT[:], bcast(ident[:].unsqueeze(1), [P, B, P])).then_inc(tt_init, 1)

            def init_cols(j):
                dve.wait_ge(nxt_done, j + 1)
                nc.vector.tensor_copy(cur[:, 0], nxt[:, 0])
                nc.vector.tensor_scalar(cur[:, 1], nxt[:, 1], -1.0, None, ALU.mult).then_inc(cur_beta, 1)

            def init_rest(j):
                dve.wait_ge(vt_done, j + 1)
                dve.wait_ge(cur_beta, j + 1)
                nc.vector.tensor_tensor(R[:], quad(b7), bcast(cur[:, 0].unsqueeze(2), [P, B, P]), ALU.mult).then_inc(vp_done, 1)
                dve.wait_ge(sums_read, j + 1)
                nc.vector.tensor_tensor(AT[:], bcast(ident[:].unsqueeze(1), [P, B, P]), bcast(qk[:].unsqueeze(2), [P, B, P]),
                                        ALU.mult).then_inc(at_init, 1)

            def body(i, h, c, hn, cn):
                j = i + 1

                def level(l):
                    n = 1 << l
                    pp = quad(b4).rearrange("p b (x m n) -> p b x m n", x=2, n=n)
                    mk = bcast(mask[:, l].rearrange("p (m n) -> p m n", n=n).unsqueeze(1), [P, B, HALF // n, n])
                    dve.wait_ge(lvl_mm, upto(l, i))
                    if l == 0:
                        dve.wait_ge(at_init, i + 1)
                    else:
                        dve.wait_ge(qk_done, upto(l - 1, i))
                    _, right = halves(NT[:, l], n)
                    nc.vector.tensor_tensor(right, pp[:, :, 0], mk, ALU.mult).then_inc(kk_done, 1)
                    _, right = halves(AT[:], n)
                    nc.vector.copy_predicated(right, mk.bitcast(U32), pp[:, :, 1]).then_inc(qk_done, 1)

                def x_scale(l):
                    n = 1 << l
                    dve.wait_ge(x_mm, upto(l, i))
                    left, _ = halves(XL[:, l], n)
                    x = halves(quad(b5), n)[0] if l == 0 else part(b5, 0, n)
                    nc.vector.tensor_tensor(left, x,
                                            bcast(cur[:, 1].unsqueeze(2).unsqueeze(3), [P, B, HALF // n, n]),
                                            ALU.mult).then_inc(x_done, 1)

                def add_t(l):
                    n = 1 << l
                    left, _ = halves(TM[:], n)
                    if l == 0:
                        dve.wait_ge(tm_init, i + 1)
                        dve.wait_ge(x_done, upto(0, i))
                        new, _ = halves(XL[:, 0], n)
                    else:
                        dve.wait_ge(t_mm, i * (LEVELS - 2) + l)
                        dve.wait_ge(t_add, upto(l - 1, i, LEVELS - 1))
                        new = part(b6, 0, n)
                    nc.vector.tensor_tensor(left, left, new, ALU.add).then_inc(t_add, 1)

                def copy_tt(l):
                    n = 1 << l
                    dve.wait_ge(tt_mm, upto(l, i))
                    if l == 0:
                        dve.wait_ge(tt_init, i + 1)
                    else:
                        dve.wait_ge(tt_copied, upto(l - 1, i))
                    _, right = halves(TT[:], n)
                    if l < LEVELS - 1:
                        _, new = halves(quad(b7), n)
                        nc.vector.tensor_copy(right, new).then_inc(tt_copied, 1)
                    else:
                        nc.vector.tensor_tensor(right, right, part(b7, 0, n), ALU.add).then_inc(tt_copied, 1)

                dve.wait_ge(nxt_done, i + 1)
                dve.wait_ge(r_ready, PRIMED + i)
                nc.vector.tensor_scalar(cur[:, 2], nxt[:, 2], 0.5, None, ALU.mult)
                nc.vector.tensor_scalar(cur[:, 3], nxt[:, 3], 1.0 / DK, None, ALU.mult).then_inc(cur_done, 1)
                level(0)
                x_scale(0)
                add_t(0)
                level(1)
                copy_tt(0)
                x_scale(1)
                level(2)
                add_t(1)
                f_low(j)
                copy_tt(1)
                x_scale(2)
                level(3)
                add_t(2)
                conv(0, j, hn, (1, 2))
                copy_tt(2)
                x_scale(3)
                level(4)
                add_t(3)
                conv(0, j, hn, (3,))
                copy_tt(3)
                x_scale(4)
                level(5)
                add_t(4)
                conv(1, j, hn, (1, 2))
                copy_tt(4)
                x_scale(5)
                level(6)
                add_t(5)
                conv(1, j, hn, (3,))
                copy_tt(5)
                x_scale(6)
                dve.wait_ge(y_mm, i + 1)
                dve.wait_ge(vp_done, i + 1)
                for b in range(B):
                    ins = nc.vector.scalar_tensor_tensor(R[:, b], quad(b4)[:, b], cur[:, 1, b:b + 1], R[:, b], ALU.mult, ALU.add)
                ins.then_inc(r_done, 1)
                copy_tt(6)
                sums(j)
                conv(2, j, hn)
                init_k(j)
                init_t(j)
                dve.wait_ge(o2_done, PRIMED + i + 1)
                dve.wait_ge(gate_done, i + 1)
                nc.vector.scalar_tensor_tensor(G[:], gt[:], 1.0, quad(b6), ALU.add, ALU.mult).then_inc(g_done, 1)
                dve.wait_ge(s_mm, i + 1)
                dve.wait_ge(lvl_upd, upto(6, i))
                dve.wait_ge(blk_done, upto(6, i))
                p128 = PB[:, B * (P - 2):B * (P - 1)]
                for b in range(B):
                    ins = nc.vector.scalar_tensor_tensor(S[:, b], S[:, b], p128[:, b:b + 1], quad(b4)[:, b], ALU.mult, ALU.add)
                ins.then_inc(s_done, 1)
                init_cols(j)
                dve.wait_ge(osum_mm, PRIMED + i + 1)
                dve.wait_ge(cur_done, i + 1)
                nc.vector.tensor_tensor(rr[:, 0], sums_o, cur[:, 3], ALU.mult).then_inc(ms_done, 1)
                dve.wait_ge(ms_done, PRIMED + i + 1)
                nc.vector.tensor_scalar(rr[:, 0], rr[:, 0], EPS_NORM, None, ALU.add).then_inc(ms_eps, 1)
                init_rest(j)
                dve.wait_ge(out_mm, i + 1)
                dve.wait_ge(r_ready, PRIMED + i + 1)
                for b in range(B):
                    bank = (b5, b6)[b // 2]
                    o = acc[:, c, b, :]
                    ins = nc.vector.scalar_tensor_tensor(o, bank[:, (b % 2) * D:(b % 2 + 1) * D], rr[:, 2, b:b + 1], o,
                                                         ALU.mult, ALU.add)
                    if b % 2:
                        ins.then_inc(acc_done, 1)

            dve.wait_ge(s_const, 1)
            over_quads(dve, prologue, body)

            def carry_wait():
                nc.vector.memset(scrap[:], 0.0)

            def normed(src, dst, st, ag, ep, rs, done, g):
                for b in range(B):
                    nc.vector.bn_stats(stats[:, b], src[:, b]).then_inc(st, 1)
                dve.wait_ge(st, B * (g + 1))
                carry_wait()
                for b in range(B):
                    nc.vector.bn_aggr(mv[:, b], stats[:, b]).then_inc(ag, 1)
                dve.wait_ge(ag, B * (g + 1))
                nc.vector.tensor_scalar(rstd[:], mv[:, :, 1], EPS_LN, None, ALU.add).then_inc(ep, 1)
                dve.wait_ge(rs, g + 1)
                for b in range(B):
                    nc.vector.tensor_scalar(dst[:, b], src[:, b], mv[:, b, 0:1], rstd[:, b:b + 1], ALU.subtract, ALU.mult
                                            ).then_inc(done, 1)

            with dve.Fori(0, NCH) as g:
                dve.wait_ge(m_x, 16 * (g + 1))
                dve.wait_ge(m_seed, PRIMED + g)
                dve.wait_ge(acc_done, PRIMED + 2 * H * NCH)
                nc.vector.tensor_tensor(x1[:], xn[:], acc[:, g], ALU.add).then_inc(m_y, 1)
                dve.wait_ge(m_y, g + 1)
                normed(x1, x1, m_st, m_ag, m_ep, m_rs, m_x1, g)
                dve.wait_ge(m_lg, g + 1)
                nc.vector.tensor_tensor(logit, b4[:, 0:B * E].rearrange("p (b e) -> p b e", b=B),
                                        bcast(rbias[:].unsqueeze(1), [P, B, E]), ALU.add).then_inc(m_lb, 1)
                dve.wait_ge(m_lb, g + 1)
                nc.vector.reduce_max(nmax[:], logit, mybir.AxisListType.X).then_inc(m_mx, 1)
                dve.wait_ge(m_mx, g + 1)
                nc.vector.tensor_scalar(nmax[:], nmax[:], -1.0, None, ALU.mult).then_inc(m_nm, 1)
                dve.wait_ge(m_ex, B * (g + 1))
                nc.vector.reciprocal(den[:, 1], den[:, 0]).then_inc(m_rc, 1)
                dve.wait_ge(m_rc, g + 1)
                nc.vector.tensor_tensor(logit, logit, bcast(den[:, 1].unsqueeze(2), [P, B, E]), ALU.mult).then_inc(m_pr, 1)
                dve.wait_ge(m_pr, g + 1)
                carry_wait()
                for b in range(B):
                    nc.vector.max(top[:, b], logit[:, b]).then_inc(m_tp, 1)
                dve.wait_ge(m_tp, B * (g + 1))
                carry_wait()
                for b in range(B):
                    nc.vector.max_index(topi[:, b], top[:, b], logit[:, b]).then_inc(m_ti, 1)
                dve.wait_ge(m_ti, B * (g + 1))
                nc.vector.tensor_copy(topf, topi).then_inc(m_tf, 1)
                nc.vector.tensor_tensor(tsum[:], top[:, :, 0], top[:, :, 1], ALU.add).then_inc(m_ts, 1)
                dve.wait_ge(m_ts, g + 1)
                nc.vector.tensor_scalar(tsum[:], tsum[:], EPS_TOPK, None, ALU.add).then_inc(m_te, 1)
                dve.wait_ge(m_te, g + 1)
                nc.vector.reciprocal(tsum[:], tsum[:]).then_inc(m_tr2, 1)
                dve.wait_ge(m_tr2, g + 1)
                nc.vector.tensor_tensor(tw[:], top[:, :, 0:2], bcast(tsum[:].unsqueeze(2), [P, B, 2]), ALU.mult).then_inc(m_tw, 1)
                dve.wait_ge(m_tw, g + 1)
                dve.wait_ge(m_tf, g + 1)
                for x, s in ((0, m_s0), (1, m_s1)):
                    for b in range(B):
                        nc.vector.tensor_scalar(wsel[:, x, b], iot[:], topf[:, b, x:x + 1], tw[:, b, x:x + 1],
                                                ALU.is_equal, ALU.mult).then_inc(s, 1)
                dve.wait_ge(m_s0, B * (g + 1))
                dve.wait_ge(m_s1, B * (g + 1))
                nc.vector.tensor_tensor(wexp[:, 0:E].rearrange("p e b -> p b e"), wsel[:, 0], wsel[:, 1], ALU.add).then_inc(m_we, 1)
                dve.wait_ge(m_we, g + 1)

                n0 = g * (E + 1)
                dve.wait_ge(silu_e, n0 + 1)
                dve.wait_ge(ht_mm, PRIMED + n0)
                for b in range(B):
                    ins = nc.vector.scalar_tensor_tensor(hw[0][:, b], sg[0][:, b], wexp[:, 0, b:b + 1], gu[0][:, b, I:2 * I],
                                                         ALU.mult, ALU.mult)
                ins.then_inc(h_e, 1)
                with dve.Fori(0, E // 2) as e2:
                    for s in range(2):
                        n = n0 + e2 * 2 + s
                        dve.wait_ge(silu_e, n + 2)
                        dve.wait_ge(ht_mm, PRIMED + n)
                        for b in range(B):
                            ins = nc.vector.scalar_tensor_tensor(hw[1 - s][:, b], sg[1 - s][:, b],
                                                                 wexp[:, e2 * 2 + (s + 1), b:b + 1],
                                                                 gu[1 - s][:, b, I:2 * I], ALU.mult, ALU.mult)
                        ins.then_inc(h_e, 1)
                dve.wait_ge(m_fin, g + 1)
                dve.wait_ge(m_out, PRIMED + 16 * g)
                for half in range(2):
                    ins = nc.vector.tensor_copy(yo[:, 2 * half:2 * half + 2].rearrange("p b n -> p (b n)"), (b5, b6)[half][:])
                ins.then_inc(m_s2, 1)
                dve.wait_ge(m_s2, PRIMED + g + 1)
                normed(yo, yo, m_st2, m_ag2, m_ep2, m_rs2, m_yo, g)

        @block.tensor
        def _(pe):
            def mm(o, l, r, start=True, stop=True, **kw):
                return nc.tensor.matmul(o, l, r, start=start, stop=stop, **kw)

            pe.wait_ge(s_ld, 16 * 13)
            pe.wait_ge(s_const, 1)
            mm(b4[:, 0:H], onesrow, alog)
            for k in range(KT):
                ins = nc.tensor.transpose(b4[:, 64 + k * E:64 + (k + 1) * E], wrn[:, k * P:(k + 1) * P], ident[0:E, 0:E])
            ins.then_inc(s_apm, 1)
            bw = U[:, 0, 0:KT * H].rearrange("p (k h) -> p k h", k=KT)
            with pe.Fori(0, NCH) as c:
                pe.wait_ge(s_xin, 16 * (c + 1))
                pe.wait_ge(s_xcp, PRIMED + c)
                for k in range(KT):
                    for b in range(B):
                        ins = nc.tensor.transpose(pj[:, 0, k, b * P:(b + 1) * P], xnat[:, b, k * P:(k + 1) * P], ident[:])
                ins.then_inc(s_xtr, 1)
                pe.wait_ge(s_xcp, PRIMED + c + 1)
                pe.wait_ge(s_xfc, PRIMED + c)
                for bank, w in ((b5, 0), (b6, 2)):
                    for k in range(KT):
                        ins = mm(bank[:], R[:, w + k], xs[:, k * 512:(k + 1) * 512], start=(k == 0), stop=(k == KT - 1))
                ins.then_inc(s_xfm, 1)
                pe.wait_ge(s_bc, PRIMED + c)
                pe.wait_ge(s_xtc, c + 1)
                for b in range(B):
                    for k in range(KT):
                        ins = mm(b7[:, b * H:(b + 1) * H], xs[:, k * 512 + b * P:k * 512 + (b + 1) * P], bw[:, k],
                                 start=(k == 0), stop=(k == KT - 1))
                ins.then_inc(s_bm, 1)
            pe.wait_ge(s_bc, PRIMED + NCH)
            pe.wait_ge(s_chain["act"], 4)

            def proj(x, j, h, c, pairs=(0, 1)):
                if 0 in pairs:
                    pe.wait_ge(w_loaded[x], 16 * h + 16)
                    if x == 0:
                        wait(pe, conv_done[2], j)
                    elif x == 1:
                        pe.wait_ge(f_relu, j + 1)
                        wait(pe, gate_done, j)
                    elif x == 2:
                        pe.wait_ge(conv_done[0], j + 1)
                for two in pairs:
                    for k in range(KT):
                        ins = mm(pair[x % 2][:, 2 * two:2 * two + 2, 0:W], wqkv[:, x, k], xT[:, k, c, 2 * two:2 * two + 2, :],
                                 start=(k == 0), stop=(k == KT - 1))
                if 1 in pairs:
                    ins.then_inc(proj_done[x], 1)

            def proj_f(j, h, c):
                pe.wait_ge(w_loaded[3], 16 * h + 16)
                wait(pe, ms_done, PRIMED + j - 1)
                mm(bank_f, wf2[:], xf[:, c]).then_inc(proj_done[3], 1)

            def proj_g(j, h, c):
                pe.wait_ge(w_loaded[4], 16 * h + 16)
                pe.wait_ge(conv_done[1], j + 1)
                mm(bank_g, wg2[:], xg[:, c]).then_inc(proj_done[4], 1)

            def sums(x, j):
                src, there = ((sq[:, 0], sq_done[0]), (sq[:, 1], sq_done[1]), (fsp[:, 2], qk_prod))[x]
                pe.wait_ge(conv_done[1], j + 1)
                pe.wait_ge(there, j + 1)
                for b in range(B):
                    ins = mm(sums_qk[:, x, b:b + 1], src[:, b], ones[:])
                if x == 2:
                    ins.then_inc(sums_done, 1)

            def v_turned(j):
                pe.wait_ge(silu_done[2], j + 1)
                for b in range(B):
                    ins = nc.tensor.transpose(quad(b7)[:, b], qkd[:, 2, b], ident[:])
                ins.then_inc(vt_done, 1)

            def prologue(j, h, c):
                proj_f(j, h, c)
                proj(0, j, h, c)
                proj(1, j, h, c)
                proj(2, j, h, c)
                proj_g(j, h, c)
                for x in range(3):
                    sums(x, j)
                v_turned(j)

            def body(i, h, c, hn, cn):
                j = i + 1

                def level(l):
                    n = 1 << l
                    if l == 0:
                        pe.wait_ge(init_done, i + 1)
                        pe.wait_ge(kr_init, i + 1)
                        pe.wait_ge(s_done, PRIMED + i)
                    else:
                        pe.wait_ge(lvl_upd, upto(l - 1, i))
                        pe.wait_ge(qk_done, upto(l - 1, i))
                    right = FQ[:].rearrange("p x b (m two n) -> p x b m two n", two=2, n=n)[:, :, :, :, 1, :]
                    for b in range(B):
                        ins = mm(quad(b4)[:, b], KR[:, b], right[:, :, b])
                    ins.then_inc(lvl_mm, 1)

                def x_(l):
                    n = 1 << l
                    pe.wait_ge(kk_done, upto(l, i))
                    if l == 0:
                        pe.wait_ge(acc_done, PRIMED + 2 * i)
                        for b in range(B):
                            ins = nc.tensor.transpose(quad(b5)[:, b], NT[:, 0, b], ident[:])
                    else:
                        pe.wait_ge(t_add, upto(l - 1, i, LEVELS - 1))
                        left, _ = halves(TM[:], n)
                        for b in range(B):
                            ins = mm(part(b5, 0, n)[:, b], NT[:, l, b], left[:, b])
                    ins.then_inc(x_mm, 1)

                def t_(l):
                    n = 1 << l
                    pe.wait_ge(x_done, upto(l, i))
                    pe.wait_ge(tt_copied, upto(l - 1, i))
                    left, _ = halves(XL[:, l], n)
                    for b in range(B):
                        ins = mm(part(b6, 0, n)[:, b], TT[:, b], left[:, b])
                    ins.then_inc(t_mm, 1)

                def tt_(l):
                    if l == 0:
                        pe.wait_ge(vp_done, i + 1)
                    else:
                        pe.wait_ge(tt_copied, upto(l - 1, i))
                    if l < LEVELS - 1:
                        pe.wait_ge(t_add, upto(l, i, LEVELS - 1))
                        for b in range(B):
                            ins = nc.tensor.transpose(quad(b7)[:, b], TM[:, b], ident[:])
                    else:
                        pe.wait_ge(x_done, upto(l, i))
                        _, right = halves(TT[:], 1 << l)
                        for b in range(B):
                            ins = mm(part(b7, 0, 1 << l)[:, b], XL[:, l, b], right[:, b])
                    ins.then_inc(tt_mm, 1)

                level(0)
                proj_f(j, hn, cn)
                proj(0, j, hn, cn, (0,))
                x_(0)
                level(1)
                tt_(0)
                x_(1)
                level(2)
                t_(1)
                proj(0, j, hn, cn, (1,))
                tt_(1)
                x_(2)
                level(3)
                t_(2)
                proj(1, j, hn, cn, (0,))
                tt_(2)
                x_(3)
                level(4)
                t_(3)
                proj(1, j, hn, cn, (1,))
                tt_(3)
                x_(4)
                level(5)
                t_(4)
                proj(2, j, hn, cn, (0,))
                tt_(4)
                x_(5)
                level(6)
                t_(5)
                proj(2, j, hn, cn, (1,))
                pe.wait_ge(lvl_upd, upto(6, i))
                pe.wait_ge(qk_done, upto(6, i))
                for b in range(B):
                    ins = nc.tensor.transpose(quad(b4)[:, b], KR[:, b], ident[:])
                ins.then_inc(krt_mm, 1)
                tt_(5)
                x_(6)
                sums(0, j)
                proj_g(j, hn, cn)
                pe.wait_ge(krt_done, i + 1)
                for b in range(B):
                    ins = mm(quad(b4)[:, b], FQ[:, 0, b], S[:, b])
                ins.then_inc(y_mm, 1)
                sums(1, j)
                tt_(6)
                sums(2, j)
                pe.wait_ge(tt_copied, upto(6, i))
                pe.wait_ge(r_done, i + 1)
                for b in range(B):
                    ins = mm(quad(b5)[:, b], TT[:, b], R[:, b])
                ins.then_inc(u_mm, 1)
                for b in range(B):
                    mm(quad(b6)[:, b], S[:, b], FQ[:, 1, b], start=(b == 0), stop=False, skip_group_check=True)
                pe.wait_ge(u_done, i + 1)
                for b in range(B):
                    ins = mm(quad(b6)[:, b], U[:, b], AT[:, b], start=False, stop=(b == B - 1), skip_group_check=True)
                ins.then_inc(o_mm, 1)
                for b in range(B):
                    ins = mm(quad(b4)[:, b], KRt[:, b], U[:, b])
                ins.then_inc(s_mm, 1)
                v_turned(j)
                pe.wait_ge(o2_done, PRIMED + i + 1)
                pe.wait_ge(sums_read, j + 1)
                for b in range(B):
                    ins = mm(sums_o[:, b:b + 1], sq[:, 0, b], ones[:])
                ins.then_inc(osum_mm, 1)
                pe.wait_ge(g_done, i + 1)
                for b in range(B):
                    ins = mm((b5, b6)[b // 2][:, (b % 2) * D:(b % 2 + 1) * D], G[:, b], ow[:, h, :])
                ins.then_inc(out_mm, 1)

            over_quads(pe, prologue, body)

            pe.wait_ge(m_w, 16 * 10)
            with pe.Fori(0, NCH) as g:
                pe.wait_ge(m_x1, B * (g + 1))
                for k in range(KT):
                    for b in range(B):
                        ins = nc.tensor.transpose(pj[:, 0, k, b * P:(b + 1) * P], x1[:, b, k * P:(k + 1) * P], ident[:])
                ins.then_inc(m_tr, 1)
                pe.wait_ge(m_s2, PRIMED + g)
                for half in range(2):
                    ins = mm((b5, b6)[half][:], ident[:], x1[:, 2 * half:2 * half + 2].rearrange("p b n -> p (b n)"),
                             start=True, stop=False, skip_group_check=True)
                ins.then_inc(m_seed, 1)
                pe.wait_ge(m_xT, g + 1)
                pe.wait_ge(ht_e, PRIMED + (E + 1) * g)
                for b in range(B):
                    for k in range(KT):
                        ins = mm(b4[:, b * E:(b + 1) * E], x1T[:, k, b * P:(b + 1) * P], wrT[:, k], start=(k == 0), stop=(k == KT - 1))
                ins.then_inc(m_lg, 1)

                def transpose_h(s, n):
                    pe.wait_ge(h_e, PRIMED + n + 1)
                    pe.wait_ge(ht_e, PRIMED + n)
                    for b in range(B):
                        ins = nc.tensor.transpose(quad(b4)[:, b], hw[s][:, b], ident[:])
                    ins.then_inc(ht_mm, 1)

                def down(e, s, n, last, done):
                    pe.wait_ge(ht_e, PRIMED + n + 1)
                    for b in range(B):
                        ins = mm((b5, b6)[b // 2][:, (b % 2) * D:(b % 2 + 1) * D], hT[s][:, b], wdn[:, e, :],
                                 start=False, stop=last, skip_group_check=True)
                    ins.then_inc(done, 1)

                n0 = g * (E + 1)
                pe.wait_ge(m_lb, g + 1)
                pe.wait_ge(h_e, PRIMED + n0)
                for b in range(B):
                    for k in range(KT):
                        ins = mm(gu[0][:, b], x1T[:, k, b * P:(b + 1) * P], wgu[:, k, 0, :], start=(k == 0), stop=(k == KT - 1))
                ins.then_inc(gu_mm, 1)
                with pe.Fori(0, E // 2) as e2:
                    for s in range(2):
                        n = n0 + e2 * 2 + s
                        pe.wait_ge(h_e, PRIMED + n)
                        for b in range(B):
                            for k in range(KT):
                                ins = mm(gu[1 - s][:, b], x1T[:, k, b * P:(b + 1) * P], wgu[:, k, e2 * 2 + (s + 1), :],
                                         start=(k == 0), stop=(k == KT - 1))
                        ins.then_inc(gu_mm, 1)
                        transpose_h(s, n)
                        down(e2 * 2 + s, s, n, False, dn_mm)
                transpose_h(0, n0 + E)
                down(E, 0, n0 + E, True, m_fin)


NAMES = {"x": "L0_attn_hidden_states"}
NAMES.update({n: "L0_attn_" + n for n in (
    "q_w", "k_w", "v_w", "q_conv_w", "k_conv_w", "v_conv_w", "f_w1", "f_w2", "b_w", "A_log", "dt_bias",
    "g_w1", "g_w2", "g_b2", "o_norm_w", "o_w")})
NAMES.update({n: "L0_ffn_" + n for n in ("Wr", "bias", "Wg", "Wu", "Wd", "sWg", "sWu", "sWd")})


def kernel(**inputs):
    import concourse.bacc as bacc
    from concourse.bass_utils import run_bass_kernel_spmd

    nc = bacc.Bacc("TRN2", target_bir_lowering=False, num_devices=1)
    arrays, aps = {}, {}
    for short, name in NAMES.items():
        v = np.ascontiguousarray(inputs[name])
        arrays[f"in_{name}"] = v
        aps[short] = nc.dram_tensor(f"in_{name}", v.shape, mybir.dt.from_np(v.dtype), kind="ExternalInput").ap()
    out = nc.dram_tensor("out", (B, T, D), FP, kind="ExternalOutput").ap()
    build(nc, aps, out)
    r = run_bass_kernel_spmd(nc, [arrays], core_ids=[0])
    return r.results[0]["out"]
```

```python
from contextlib import ExitStack

import numpy as np

import concourse.bass as bass
from concourse import mybir

FP = mybir.dt.float32
U32 = mybir.dt.uint32
ALU = mybir.AluOpType
ACT = mybir.ActivationFunctionType

B, T, D = 4, 1024, 256
H, DK = 16, 128
P = 128
KT = D // P
NCH = T // P
TAPS = 4
HALO = TAPS - 1
W = P + HALO
LEVELS = 7
HALF = P // 2
PRIMED = 1
E = 16
I = 128
EPS_NORM, EPS_L2, EPS_TOPK, EPS_LN = 1e-5, 1e-6, 1e-9, 1e-5


def build(nc, a, out):
    ctx = ExitStack()
    with ctx:
        def sb(name, shape, dt=FP):
            return ctx.enter_context(nc.sbuf_tensor(name, shape, dt))

        def ps(name):
            return ctx.enter_context(nc.psum_tensor(name, [P, 512], FP))

        def sem(name):
            return ctx.enter_context(nc.semaphore(name))

        def sems(name, n):
            return [sem(f"{name}{k}") for k in range(n)]

        XT = KT * (NCH + 1) * B * W
        XF = NCH * B * P
        arena = sb("arena", [P, XT + 2 * XF])
        xT = arena[:, 0:XT].rearrange("p (k c b w) -> p k c b w", k=KT, c=NCH + 1, b=B)
        xf = arena[:, XT:XT + XF].rearrange("p (c n) -> p c n", c=NCH)
        xg = arena[:, XT + XF:XT + 2 * XF].rearrange("p (c n) -> p c n", c=NCH)
        wgu = arena[:, 0:KT * (E + 1) * 2 * I].rearrange("p (k e n) -> p k e n", k=KT, e=E + 1)
        wdn = arena[:, KT * (E + 1) * 2 * I:(KT * 2 * I + D) * (E + 1)].rearrange("p (e n) -> p e n", e=E + 1)
        acc = sb("acc", [P, NCH, B, D])
        ow = sb("ow", [P, H, D])
        wqkv = sb("wqkv", [P, 3, KT, DK])
        wf2 = sb("wf2", [P, DK])
        wg2 = sb("wg2", [P, DK])
        convw = sb("convw", [P, 3, H + 1, TAPS])
        dtb = sb("dtb", [P, H + 1])
        gb2h = sb("gb2h", [P, H + 1])
        negA = sb("negA", [P, H + 1])
        beta = sb("beta", [P, H + 1, NCH, B])
        onw = sb("onw", [P, 1])
        ident = sb("ident", [P, P])
        ones = sb("ones", [P, 1])
        keep = sb("keep", [P, NCH])
        mhalf = sb("mhalf", [P, 16])
        mask = sb("mask", [P, LEVELS, HALF])
        qkd = sb("qkd", [P, 4, B, P])
        pre = sb("pre", [P, 2, B, P])
        sq = sb("sq", [P, 2, B, P])
        fsp = sb("fsp", [P, 4, B, P])
        FQ = sb("FQ", [P, 2, B, P])
        KR = sb("KR", [P, B, P])
        PB = sb("PB", [P, B * (P - 1)])
        NT = sb("NT", [P, LEVELS, B, P])
        XL = sb("XL", [P, LEVELS, B, P])
        TM = sb("TM", [P, B, P])
        TT = sb("TT", [P, B, P])
        AT = sb("AT", [P, B, P])
        R = sb("R", [P, B, P])
        U = sb("U", [P, B, P])
        KRt = sb("KRt", [P, B, P])
        S = sb("S", [P, B, P])
        gt = sb("gt", [P, B, P])
        G = sb("G", [P, B, P])
        onesrow, alog = KRt[0:1, 0], KRt[0:1, 1, 0:H]
        nxt = sb("nxt", [P, 4, B])
        cur = sb("cur", [P, 4, B])
        qk = sb("qk", [P, B])
        ssum = sb("ssum", [P, 2, B])
        sinv = sb("sinv", [P, 2, B])
        rr = sb("rr", [P, 3, B])
        flatN = NT[:].rearrange("p l b n -> p (l b n)")
        flatZ = XL[:].rearrange("p l b n -> p (l b n)")
        xn = flatN[:, 0:1024].rearrange("p (b n) -> p b n", b=B)
        x1 = flatN[:, 1024:2048].rearrange("p (b n) -> p b n", b=B)
        x1T = flatN[:, 2048:3072].rearrange("p (k n) -> p k n", k=KT)
        yo = flatZ[:, 0:1024].rearrange("p (b n) -> p b n", b=B)
        yn = flatZ[:, 1024:2048].rearrange("p (b n) -> p b n", b=B)
        sg = [flatZ[:, 2048 + 512 * s:2560 + 512 * s].rearrange("p (b n) -> p b n", b=B) for s in range(2)]
        hT = [qkd[:, s] for s in range(2)]
        scrap = sb("scrap", [P, 1])
        stats = sb("stats", [P, B, 6])
        mv = sb("mv", [P, B, 2])
        rstd = sb("rstd", [P, B])
        wrn = G[0:E, 0:2].rearrange("p a n -> p (a n)")
        wrT = sb("wrT", [P, KT, E])
        rbias = sb("rbias", [P, E])
        logit = AT[:, 0, 0:B * E].rearrange("p (b e) -> p b e", b=B)
        nmax = sb("nmax", [P, B])
        den = sb("den", [P, 2, B])
        top, topi, topf = (AT[:, 2, 8 * B * x:8 * B * (x + 1)].rearrange("p (b n) -> p b n", b=B) for x in range(3))
        topi = topi.bitcast(U32)
        tsum = sb("tsum", [P, B])
        tw = sb("tw", [P, B, 2])
        iot = sb("iot", [P, E])
        wsel = AT[:, 1, 0:2 * B * E].rearrange("p (x b e) -> p x b e", x=2, b=B)
        wexp = sb("wexp", [P, E + 1, B])

        pj = ctx.enter_context(nc.psum_tensor("pj", [P, 2, 2, 512], FP))
        b4, b5, b6, b7 = ps("b4"), ps("b5"), ps("b6"), ps("b7")

        def quad(bank):
            return bank[:, 0:512].rearrange("p (b n) -> p b n", b=B)

        pair = [pj[:, n].rearrange("p a (x w) -> p (a x) w", x=2) for n in range(2)]
        xnat = pre[:].rearrange("p a b n -> p (a b n)").rearrange("p (b n) -> p b n", b=B)
        xs = fsp[:, 0:2].rearrange("p a b n -> p (a b n)")
        gu = [[quad(pj[:, n, x]) for x in range(2)] for n in range(2)]
        dn = [[bank[:].rearrange("p (b n) -> p b n", b=2) for bank in two] for two in ((b4, b5), (b6, b7))]
        x1t = pj[:, 1].rearrange("p k n -> p (k n)").rearrange("p (k n) -> p k n", k=KT)
        lgt = pj[:, 1, 0, 0:B * E].rearrange("p (b e) -> p b e", b=B)
        bank_f, bank_g = pj[:, 1, 0], pj[:, 1, 1]
        sums_qk = bank_f[:, 0:3 * B].rearrange("p (x b) -> p x b", x=3)
        sums_o = bank_f[:, 3 * B:4 * B]

        def halves(ap, n):
            v = ap.rearrange("p b (m two n) -> p b m two n", two=2, n=n)
            return v[:, :, :, 0, :], v[:, :, :, 1, :]

        def part(bank, lo, n):
            return bank[:, lo:lo + B * HALF].rearrange("p (b m n) -> p b m n", b=B, n=n)

        s_const = sem("s_const")
        s_chain = {k: sem(f"s_chain_{k}") for k in ("pool", "act")}
        s_ld = sem("s_ld")
        s_xin, s_xtr, s_xcp, s_xtc, s_xfm, s_xfc = (sem(n) for n in ("s_xin", "s_xtr", "s_xcp", "s_xtc", "s_xfm", "s_xfc"))
        s_bm, s_bc, s_apm = sem("s_bm"), sem("s_bc"), sem("s_apm")
        w_loaded = sems("w_loaded", 5)
        proj_done = sems("proj_done", 5)
        tap_done = sems("tap_done", 3)
        conv_step = sems("conv_step", 3)
        conv_done = sems("conv_done", 3)
        silu_done = sems("silu_done", 3)
        sq_done = sems("sq_done", 2)
        qk_prod = sem("qk_prod")
        sums_done, sums_read, inv_done, nxt1, nxt_done, cur_done = (
            sem(n) for n in ("sums_done", "sums_read", "inv_done", "nxt1", "nxt_done", "cur_done"))
        cur_beta = sem("cur_beta")
        f_abs, f_relu, f_exp, f_ln, f_w1, f_sub, f_add, f_sum, d_exp, d_done, gate_done = (
            sem(n) for n in ("f_abs", "f_relu", "f_exp", "f_ln", "f_w1", "f_sub", "f_add", "f_sum", "d_exp", "d_done", "gate_done"))
        init_done, tm_init, tt_init, vt_done, at_init, vp_done = (
            sem(n) for n in ("init_done", "tm_init", "tt_init", "vt_done", "at_init", "vp_done"))
        x_mm, x_done, t_mm, t_add, kr_init = (sem(n) for n in ("x_mm", "x_done", "t_mm", "t_add", "kr_init"))
        lvl_mm = sem("lvl_mm")
        blk_done = sem("blk_done")
        lvl_upd = sem("lvl_upd")
        kk_done = sem("kk_done")
        qk_done = sem("qk_done")
        tt_mm = sem("tt_mm")
        tt_copied = sem("tt_copied")
        krt_mm, krt_done, y_mm, r_done, u_mm, u_done, o_mm, s_mm, s_done = (
            sem(n) for n in ("krt_mm", "krt_done", "y_mm", "r_done", "u_mm", "u_done", "o_mm", "s_mm", "s_done"))
        g_done, o2_done, osum_mm, ms_done, ms_eps, ms_pow, r_ready, out_mm, acc_done = (
            sem(n) for n in ("g_done", "o2_done", "osum_mm", "ms_done", "ms_eps", "ms_pow", "r_ready", "out_mm", "acc_done"))
        m_w = sem("m_w")
        (m_x, m_y, m_st, m_ag, m_ep, m_rs, m_x1, m_tr, m_xT, m_lg, m_lb, m_mx, m_nm, m_ex, m_rc, m_pr, m_tp, m_ti, m_tf,
         m_ts, m_te, m_tr2, m_tw, m_s0, m_s1, m_we, m_st2, m_ag2, m_ep2, m_rs2, m_yn, m_out) = (
            sem(n) for n in ("m_x m_y m_st m_ag m_ep m_rs m_x1 m_tr m_xT m_lg m_lb m_mx m_nm m_ex m_rc m_pr m_tp m_ti m_tf "
                             "m_ts m_te m_tr2 m_tw m_s0 m_s1 m_we m_st2 m_ag2 m_ep2 m_rs2 m_yn m_out").split())
        gu_mm, silu_e, h_e, dn_mm, sum_e = (sem(n) for n in ("gu_mm", "silu_e", "h_e", "dn_mm", "sum_e"))

        def wait(eng, s, value):
            if isinstance(value, int) and value <= 0:
                return
            eng.wait_ge(s, value)

        def upto(l, i, levels=LEVELS):
            return i * levels + (l + 1)

        def over_quads(eng, stage_a, body):
            stage_a(0, 0, 0)
            with eng.Fori(0, H) as h:
                with eng.Fori(0, NCH - 1) as c:
                    body(h * NCH + c, h, c, h, c + 1)
                body(h * NCH + (NCH - 1), h, NCH - 1, h + 1, 0)

        def bcast(ap, shape):
            return ap.to_broadcast(shape)

        block = ctx.enter_context(nc.Block())
        names = ("q", "k", "v")

        @block.sync
        def _(sp):
            for s in (o_mm, r_ready, acc_done, s_done, o2_done, osum_mm, ms_done, s_bm, s_xcp, s_xfc, s_bc, m_out,
                      h_e, dn_mm, sum_e):
                sp.sem_inc(s, PRIMED)
            n = 0
            for dst, src in (
                (convw[:, 0, 0:H], a["q_conv_w"].rearrange("(h p) t -> p h t", p=P)),
                (convw[:, 1, 0:H], a["k_conv_w"].rearrange("(h p) t -> p h t", p=P)),
                (convw[:, 2, 0:H], a["v_conv_w"].rearrange("(h p) t -> p h t", p=P)),
                (dtb[:, 0:H], a["dt_bias"].rearrange("(h p) -> p h", p=P)),
                (gb2h[:, 0:H], a["g_b2"].rearrange("(h p) -> p h", p=P)),
                (alog, a["A_log"].rearrange("(o h) -> o h", o=1)),
                (onw[:], a["o_norm_w"].rearrange("(p o) -> p o", o=1)),
                (ow[:], a["o_w"].rearrange("(h p) n -> p h n", p=P)),
                (wrn, a["Wr"]),
                (R[:, 0:2], a["f_w1"].rearrange("(k p) n -> p k n", p=P)),
                (R[:, 2:4], a["g_w1"].rearrange("(k p) n -> p k n", p=P)),
                (U[:, 0, 0:KT * H].rearrange("p (k h) -> p k h", k=KT), a["b_w"].rearrange("(k p) n -> p k n", p=P)),
                (rbias[:], a["bias"].partition_broadcast(P)),
            ):
                sp.dma_start(dst, src, allow_slow_non_contiguous=True).then_inc(s_ld, 16)
                n += 1

            def weights(h, prev):
                for x, name in enumerate(("q_w", "k_w", "v_w")):
                    wait(sp, proj_done[x], prev)
                    sp.dma_start(wqkv[:, x], a[name].rearrange("(k p) (h n) -> p k h n", p=P, n=DK)[:, :, h, :]
                                 ).then_inc(w_loaded[x], 16)
                for x, (dst, name) in enumerate(((wf2, "f_w2"), (wg2, "g_w2"))):
                    wait(sp, proj_done[3 + x], prev)
                    sp.dma_start(dst[:], a[name].rearrange("p (h n) -> p h n", n=DK)[:, h, :]).then_inc(w_loaded[3 + x], 16)

            xsrc = a["x"].rearrange("b (c p) d -> p c b d", p=P)
            sp.dma_start(xnat, xsrc[:, 0]).then_inc(s_xin, 16)
            weights(0, 0)
            with sp.Fori(1, NCH) as c:
                sp.wait_ge(s_xtr, c)
                sp.dma_start(xnat, xsrc[:, c]).then_inc(s_xin, 16)
            with sp.Fori(1, H) as h:
                weights(h, h * NCH)
            weights(0, H * NCH)

            sp.wait_ge(proj_done[4], H * NCH + 1)
            for k in range(KT):
                for x, (name, shared) in enumerate((("Wg", "sWg"), ("Wu", "sWu"))):
                    sp.dma_start(wgu[:, k, 0:E, x * I:(x + 1) * I],
                                 a[name].rearrange("e (k p) n -> p k e n", p=P)[:, k]).then_inc(m_w, 16)
                    sp.dma_start(wgu[:, k, E, x * I:(x + 1) * I],
                                 a[shared].rearrange("(k p) n -> p k n", p=P)[:, k]).then_inc(m_w, 16)
            sp.dma_start(wdn[:, 0:E], a["Wd"].rearrange("e p n -> p e n")).then_inc(m_w, 16)
            sp.dma_start(wdn[:, E], a["sWd"]).then_inc(m_w, 16)
            sp.wait_ge(out_mm, H * NCH)
            odst = out.rearrange("b (c p) d -> p c b d", p=P)
            sp.dma_start(xn, xsrc[:, 0]).then_inc(m_x, 16)

            with sp.Fori(1, NCH) as g:
                sp.wait_ge(m_y, g)
                sp.dma_start(xn, xsrc[:, g]).then_inc(m_x, 16)
                sp.wait_ge(m_yn, B * g)
                sp.dma_start(odst[:, g - 1], yn).then_inc(m_out, 16)
            sp.wait_ge(m_yn, B * NCH)
            sp.dma_start(odst[:, NCH - 1], yn).then_inc(m_out, 16)
            sp.wait_ge(m_out, PRIMED + 16 * NCH)

        @block.gpsimd
        def _(pool):
            cnt = [0]

            def link(ins):
                cnt[0] += 1
                ins.then_inc(s_chain["pool"], 1)
                pool.wait_ge(s_chain["pool"], cnt[0])

            for t, v in ((ident[:], 0.0), (ones[:], 1.0), (onesrow, 1.0), (keep[:], 1.0), (mhalf[:], -0.5),
                         (mask[:], 1.0), (NT[:], 0.0), (XL[:], 0.0), (S[:], 0.0),
                         (xT[:, :, 0, :, 0:HALO], 0.0), (convw[:, :, H], 0.0), (dtb[:, H:H + 1], 0.0),
                         (gb2h[:, H:H + 1], 0.0), (negA[:, H:H + 1], 0.0), (beta[:, H], 0.0), (wexp[:, E], 1.0)):
                link(nc.gpsimd.memset(t, v))
            link(nc.gpsimd.memset(keep[:, 0:1], 0.0))
            link(nc.gpsimd.iota(topi[:, 0:2, :].rearrange("p b n -> p (b n)").bitcast(mybir.dt.int32), [[1, E]], base=0, channel_multiplier=0))
            link(nc.gpsimd.tensor_copy(iot[:], topi[:, 0:2, :].rearrange("p b n -> p (b n)").bitcast(mybir.dt.int32)))
            link(nc.gpsimd.affine_select(out=ident[:], in_=ident[:], compare_op=ALU.not_equal, fill=1.0, base=0,
                                         pattern=[[-1, P]], channel_multiplier=1))
            for l in range(LEVELS):
                n = 1 << l
                m = HALF // n
                v = mask[:, l].rearrange("p (m n) -> p m n", n=n)
                link(nc.gpsimd.affine_select(out=v, in_=v, compare_op=ALU.is_ge, fill=0.0, base=0,
                                             pattern=[[-2 * n, m], [0, n]], channel_multiplier=1))
                link(nc.gpsimd.affine_select(out=v, in_=v, compare_op=ALU.is_ge, fill=0.0, base=n - 1,
                                             pattern=[[2 * n, m], [0, n]], channel_multiplier=-1))
            nc.gpsimd.memset(acc[:], 0.0).then_inc(s_const, 1)

            off = [0]
            for l in range(LEVELS):
                off.append(off[-1] + B * (HALF >> l))

            def blocks(l):
                if l == 0:
                    return qkd[:, 3].rearrange("p b n -> p (b n)")
                return PB[:, off[l - 1]:off[l]]

            def softplus_add(j):
                pool.wait_ge(f_relu, j + 1)
                pool.wait_ge(f_sub, j + 1)
                nc.gpsimd.tensor_tensor(fsp[:, 3], fsp[:, 3], fsp[:, 0], ALU.add).then_inc(f_add, 1)

            def softplus_sum(j):
                pool.wait_ge(f_add, j + 1)
                pool.wait_ge(f_ln, j + 1)
                nc.gpsimd.tensor_tensor(fsp[:, 3], fsp[:, 3], fsp[:, 2], ALU.add).then_inc(f_sum, 1)

            def stage_a_prod(j):
                pool.wait_ge(silu_done[1], j + 1)
                nc.gpsimd.tensor_tensor(fsp[:, 2], qkd[:, 0], qkd[:, 1], ALU.mult).then_inc(qk_prod, 1)

            def stage_a_cols(j, h, c):
                pool.wait_ge(sums_read, j + 1)
                nc.gpsimd.tensor_tensor(sinv[:], ssum[:], mhalf[:, 0:2 * B].rearrange("p (x b) -> p x b", x=2), ALU.pow
                                        ).then_inc(inv_done, 1)
                pool.wait_ge(inv_done, j + 1)
                wait(pool, cur_done, j)
                nc.gpsimd.tensor_tensor(nxt[:, 0], sinv[:, 1], beta[:, h, c, :], ALU.mult).then_inc(nxt1, 1)
                nc.gpsimd.tensor_tensor(nxt[:, 3], sinv[:, 0], sinv[:, 0], ALU.mult)
                nc.gpsimd.tensor_copy(nxt[:, 2], sinv[:, 0])
                pool.wait_ge(nxt1, j + 1)
                nc.gpsimd.tensor_tensor(nxt[:, 1], nxt[:, 0], sinv[:, 1], ALU.mult).then_inc(nxt_done, 1)

            def stage_a_keep(j, h, c):
                pool.wait_ge(d_exp, j + 1)
                nc.gpsimd.tensor_tensor(qkd[:, 3, :, 0], qkd[:, 3, :, 0], bcast(keep[:, bass.ds(c, 1)], [P, B]), ALU.mult
                                        ).then_inc(d_done, 1)

            def pair_blocks(l, i):
                if l:
                    pool.wait_ge(blk_done, upto(l - 1, i))
                pl = blocks(l).rearrange("p (m two) -> p m two", two=2)
                nc.gpsimd.tensor_tensor(blocks(l + 1), pl[:, :, 0], pl[:, :, 1], ALU.mult).then_inc(blk_done, 1)

            def init(j):
                pool.wait_ge(silu_done[1], j + 1)
                pool.wait_ge(d_done, j + 1)
                pool.wait_ge(o_mm, PRIMED + j)
                nc.gpsimd.tensor_tensor(FQ[:, 0], qkd[:, 1], qkd[:, 3], ALU.mult)
                nc.gpsimd.tensor_tensor(FQ[:, 1], qkd[:, 0], qkd[:, 3], ALU.mult).then_inc(init_done, 1)
                pair_blocks(0, j)

            def prologue(j, h, c):
                pool.wait_ge(s_bc, PRIMED + NCH)
                softplus_add(j)
                softplus_sum(j)
                stage_a_keep(j, h, c)
                stage_a_prod(j)
                stage_a_cols(j, h, c)
                init(j)

            def body(i, h, c, hn, cn):
                for l in range(LEVELS):
                    n = 1 << l
                    pl = blocks(l).rearrange("p (m two) -> p m two", two=2)
                    if l:
                        pair_blocks(l, i)
                    pool.wait_ge(lvl_mm, upto(l, i))
                    if l == 0:
                        pool.wait_ge(init_done, i + 1)
                    else:
                        pool.wait_ge(lvl_upd, upto(l - 1, i))
                    kl, _ = halves(KR[:], n)
                    kl = kl.rearrange("p b m n -> p (b m) n")
                    nc.gpsimd.tensor_tensor(kl, kl, bcast(pl[:, :, 1:2], [P, B * HALF // n, n]), ALU.mult)
                    fr = FQ[:].rearrange("p x b (m two n) -> p x (b m) two n", two=2, n=n)[:, :, :, 1, :]
                    nc.gpsimd.tensor_tensor(fr, fr, bcast(pl[:, :, 0:1].unsqueeze(1), [P, 2, B * HALF // n, n]), ALU.mult
                                            ).then_inc(lvl_upd, 1)
                    if l == 2:
                        softplus_add(i + 1)
                    if l == 3:
                        softplus_sum(i + 1)
                    if l == 5:
                        stage_a_keep(i + 1, hn, cn)
                stage_a_prod(i + 1)
                stage_a_cols(i + 1, hn, cn)
                init(i + 1)
                pool.wait_ge(ms_eps, i + 1)
                nc.gpsimd.tensor_tensor(rr[:, 1], rr[:, 0], mhalf[:, 0:B], ALU.pow).then_inc(ms_pow, 1)
                pool.wait_ge(ms_pow, i + 1)
                nc.gpsimd.tensor_tensor(rr[:, 2], rr[:, 1], cur[:, 2], ALU.mult).then_inc(r_ready, 1)

            over_quads(pool, prologue, body)

            def inv_std(done, there, g):
                pool.wait_ge(there, g + 1)
                nc.gpsimd.tensor_tensor(rstd[:], rstd[:], mhalf[:, 0:B], ALU.pow).then_inc(done, 1)

            inv_std(m_rs, m_ep, 0)
            with pool.Fori(1, NCH) as g:
                inv_std(m_rs, m_ep, g)
                inv_std(m_rs2, m_ep2, g - 1)
            inv_std(m_rs2, m_ep2, NCH - 1)

        @block.scalar
        def _(act):
            act.wait_ge(s_ld, 16 * 13)
            act.wait_ge(s_const, 1)
            nc.scalar.mul(gb2h[:, 0:H], gb2h[:, 0:H], 0.5)
            act.wait_ge(s_apm, 1)
            nc.scalar.activation(negA[:, 0:H], b4[:, 0:H], ACT.Exp).then_inc(s_chain["act"], 1)
            act.wait_ge(s_chain["act"], 1)
            nc.scalar.mul(negA[:, 0:H], negA[:, 0:H], -1.0).then_inc(s_chain["act"], 1)
            nc.scalar.copy(wrT[:], b4[:, 64:64 + KT * E].rearrange("p (k e) -> p k e", k=KT)).then_inc(s_chain["act"], 1)
            nc.scalar.mul(ow[:], ow[:], onw[:]).then_inc(s_chain["act"], 1)
            act.wait_ge(s_chain["act"], 4)

            with act.Fori(0, NCH) as c:
                act.wait_ge(s_xtr, c + 1)
                act.wait_ge(s_bm, PRIMED + c)
                nc.scalar.copy(xs, pj[:, 0].rearrange("p a n -> p (a n)")).then_inc(s_xcp, 1)
                act.wait_ge(s_xfm, c + 1)
                nc.scalar.copy(xf[:, c], b5[:])
                nc.scalar.copy(xg[:, c], b6[:]).then_inc(s_xfc, 1)
                act.wait_ge(s_bm, PRIMED + c + 1)
                nc.scalar.activation(beta[:, 0:H, c, :].rearrange("p h b -> p b h"),
                                     b7[:, 0:B * H].rearrange("p (b h) -> p b h", b=B), ACT.Sigmoid).then_inc(s_bc, 1)

            def tap(x, j, h):
                act.wait_ge(proj_done[x], j + 1)
                if x == 2:
                    act.wait_ge(silu_done[0], j + 1)
                elif x == 0:
                    wait(act, silu_done[2], j)
                else:
                    wait(act, silu_done[1], j)
                nc.scalar.activation(pre[:, x % 2], pair[x % 2][:, :, 0:P], ACT.Copy, scale=convw[:, x, h, 0:1]
                                     ).then_inc(tap_done[x], 1)

            def silu(x, j):
                act.wait_ge(conv_done[x], j + 1)
                wait(act, init_done, j)
                wait(act, vt_done, j)
                wait(act, qk_prod, j)
                nc.scalar.activation(qkd[:, x], pre[:, x % 2], ACT.Silu).then_inc(silu_done[x], 1)

            def square(x, j):
                act.wait_ge(silu_done[x], j + 1)
                wait(act, sums_done, j)
                if x == 0:
                    wait(act, osum_mm, PRIMED + j - 1)
                nc.scalar.activation(sq[:, x], qkd[:, x], ACT.Square).then_inc(sq_done[x], 1)

            def f_start(j, h):
                act.wait_ge(proj_done[3], j + 1)
                wait(act, f_sum, j)
                f = quad(bank_f)
                nc.scalar.activation(fsp[:, 1], f, ACT.Abs, bias=dtb[:, bass.ds(h, 1)]).then_inc(f_abs, 1)
                nc.scalar.activation(fsp[:, 0], f, ACT.Relu, bias=dtb[:, bass.ds(h, 1)]).then_inc(f_relu, 1)

            def f_e(j):
                act.wait_ge(f_abs, j + 1)
                nc.scalar.activation(fsp[:, 1], fsp[:, 1], ACT.Exp, scale=-1.0).then_inc(f_exp, 1)

            def f_l(j):
                act.wait_ge(f_exp, j + 1)
                wait(act, sums_done, j)
                nc.scalar.activation(fsp[:, 2], fsp[:, 1], ACT.Ln, bias=1.0).then_inc(f_ln, 1)

            def f_d(j, h):
                act.wait_ge(f_sum, j + 1)
                wait(act, lvl_upd, upto(0, j - 1))
                wait(act, blk_done, upto(0, j - 1))
                nc.scalar.activation(qkd[:, 3], fsp[:, 3], ACT.Exp, scale=negA[:, bass.ds(h, 1)]).then_inc(d_exp, 1)

            def gate(j, h):
                act.wait_ge(proj_done[4], j + 1)
                wait(act, g_done, j)
                nc.scalar.activation(gt[:], quad(bank_g), ACT.Tanh, bias=gb2h[:, bass.ds(h, 1)], scale=0.5).then_inc(gate_done, 1)

            def prologue(j, h, c):
                f_start(j, h)
                f_e(j)
                f_l(j)
                tap(0, j, h)
                f_d(j, h)
                tap(1, j, h)
                silu(0, j)
                square(0, j)
                tap(2, j, h)
                silu(1, j)
                square(1, j)
                silu(2, j)
                gate(j, h)

            def body(i, h, c, hn, cn):
                j = i + 1

                f_start(j, hn)
                f_e(j)
                f_l(j)
                tap(0, j, hn)
                f_d(j, hn)
                tap(1, j, hn)
                silu(0, j)
                square(0, j)
                silu(1, j)
                square(1, j)
                tap(2, j, hn)
                act.wait_ge(krt_mm, i + 1)
                nc.scalar.copy(KRt[:], quad(b4)).then_inc(krt_done, 1)
                act.wait_ge(u_mm, i + 1)
                nc.scalar.copy(U[:], quad(b5)).then_inc(u_done, 1)
                silu(2, j)
                act.wait_ge(o_mm, PRIMED + i + 1)
                act.wait_ge(sums_done, j + 1)
                nc.scalar.activation(sq[:, 0], quad(b6), ACT.Square).then_inc(o2_done, 1)
                gate(j, hn)

            over_quads(act, prologue, body)

            def take_x1T(g):
                act.wait_ge(m_tr, g + 1)
                nc.scalar.copy(x1T, x1t).then_inc(m_xT, 1)

            def group(g, last):
                act.wait_ge(m_nm, g + 1)
                for b in range(B):
                    nc.scalar.activation(logit[:, b], logit[:, b], ACT.Exp, bias=nmax[:, b:b + 1],
                                         accum_out=den[:, 0, b:b + 1]).then_inc(m_ex, 1)
                for e in range(E + 1):
                    n = g * (E + 1) + e
                    act.wait_ge(gu_mm, n + 1)
                    wait(act, h_e, PRIMED + n - 1)
                    nc.scalar.activation(sg[e % 2], gu[e % 2][0], ACT.Silu).then_inc(silu_e, 1)
                if not last:
                    take_x1T(g + 1)

            take_x1T(0)
            with act.Fori(0, NCH - 1) as g:
                group(g, False)
            group(NCH - 1, True)

        @block.vector
        def _(dve):
            with dve.Fori(0, NCH) as c:
                dve.wait_ge(s_xcp, PRIMED + c + 1)
                v = xs.rearrange("p (k b n) -> p k b n", k=KT, b=B)
                for k in range(KT):
                    nc.vector.tensor_copy(xT[:, k, c, :, HALO:W], v[:, k])
                    ins = nc.vector.tensor_copy(xT[:, k, c + 1, :, 0:HALO], v[:, k, :, P - HALO:P])
                ins.then_inc(s_xtc, 1)

            def conv(x, j, h, taps=range(1, TAPS)):
                src = pair[x % 2]
                for t in taps:
                    if t == 1:
                        dve.wait_ge(tap_done[x], j + 1)
                    else:
                        dve.wait_ge(conv_step[x], 2 * j + t - 1)
                    nc.vector.scalar_tensor_tensor(
                        pre[:, x % 2], src[:, :, t:t + P], convw[:, x, h, t:t + 1], pre[:, x % 2], ALU.mult, ALU.add
                    ).then_inc(conv_done[x] if t == HALO else conv_step[x], 1)

            def f_low(j):
                dve.wait_ge(f_exp, j + 1)
                wait(dve, d_exp, j)
                nc.vector.tensor_scalar(fsp[:, 3], fsp[:, 1], 1.0, 1.0, ALU.add, ALU.subtract).then_inc(f_w1, 1)
                dve.wait_ge(f_w1, j + 1)
                nc.vector.tensor_tensor(fsp[:, 3], fsp[:, 1], fsp[:, 3], ALU.subtract).then_inc(f_sub, 1)

            def sums(j):
                dve.wait_ge(sums_done, j + 1)
                wait(dve, nxt_done, j)
                nc.vector.tensor_copy(qk[:], sums_qk[:, 2])
                nc.vector.tensor_scalar(ssum[:, 1], sums_qk[:, 1], EPS_L2, None, ALU.add)
                nc.vector.tensor_scalar(ssum[:, 0], sums_qk[:, 0], EPS_L2, float(DK), ALU.add, ALU.mult).then_inc(sums_read, 1)

            def prologue(j, h, c):
                f_low(j)
                conv(0, j, h)
                conv(1, j, h)
                conv(2, j, h)
                sums(j)
                init_k(j)
                init_t(j)
                init_cols(j)
                init_rest(j)

            def init_k(j):
                dve.wait_ge(silu_done[1], j + 1)
                wait(dve, krt_mm, j)
                nc.vector.tensor_copy(KR[:], qkd[:, 1]).then_inc(kr_init, 1)
                nc.vector.tensor_copy(TM[:], bcast(ident[:].unsqueeze(1), [P, B, P])).then_inc(tm_init, 1)

            def init_t(j):
                wait(dve, u_mm, j)
                nc.vector.tensor_copy(TT[:], bcast(ident[:].unsqueeze(1), [P, B, P])).then_inc(tt_init, 1)

            def init_cols(j):
                dve.wait_ge(nxt_done, j + 1)
                nc.vector.tensor_copy(cur[:, 0], nxt[:, 0])
                nc.vector.tensor_scalar(cur[:, 1], nxt[:, 1], -1.0, None, ALU.mult).then_inc(cur_beta, 1)

            def init_rest(j):
                dve.wait_ge(vt_done, j + 1)
                dve.wait_ge(cur_beta, j + 1)
                nc.vector.tensor_tensor(R[:], quad(b7), bcast(cur[:, 0].unsqueeze(2), [P, B, P]), ALU.mult).then_inc(vp_done, 1)
                dve.wait_ge(sums_read, j + 1)
                nc.vector.tensor_tensor(AT[:], bcast(ident[:].unsqueeze(1), [P, B, P]), bcast(qk[:].unsqueeze(2), [P, B, P]),
                                        ALU.mult).then_inc(at_init, 1)

            def body(i, h, c, hn, cn):
                j = i + 1

                def level(l):
                    n = 1 << l
                    pp = quad(b4).rearrange("p b (x m n) -> p b x m n", x=2, n=n)
                    mk = bcast(mask[:, l].rearrange("p (m n) -> p m n", n=n).unsqueeze(1), [P, B, HALF // n, n])
                    dve.wait_ge(lvl_mm, upto(l, i))
                    if l == 0:
                        dve.wait_ge(at_init, i + 1)
                    else:
                        dve.wait_ge(qk_done, upto(l - 1, i))
                    _, right = halves(NT[:, l], n)
                    nc.vector.tensor_tensor(right, pp[:, :, 0], mk, ALU.mult).then_inc(kk_done, 1)
                    _, right = halves(AT[:], n)
                    nc.vector.copy_predicated(right, mk.bitcast(U32), pp[:, :, 1]).then_inc(qk_done, 1)

                def x_scale(l):
                    n = 1 << l
                    dve.wait_ge(x_mm, upto(l, i))
                    left, _ = halves(XL[:, l], n)
                    x = halves(quad(b5), n)[0] if l == 0 else part(b5, 0, n)
                    nc.vector.tensor_tensor(left, x,
                                            bcast(cur[:, 1].unsqueeze(2).unsqueeze(3), [P, B, HALF // n, n]),
                                            ALU.mult).then_inc(x_done, 1)

                def add_t(l):
                    n = 1 << l
                    left, _ = halves(TM[:], n)
                    if l == 0:
                        dve.wait_ge(tm_init, i + 1)
                        dve.wait_ge(x_done, upto(0, i))
                        new, _ = halves(XL[:, 0], n)
                    else:
                        dve.wait_ge(t_mm, i * (LEVELS - 2) + l)
                        dve.wait_ge(t_add, upto(l - 1, i, LEVELS - 1))
                        new = part(b6, 0, n)
                    nc.vector.tensor_tensor(left, left, new, ALU.add).then_inc(t_add, 1)

                def copy_tt(l):
                    n = 1 << l
                    dve.wait_ge(tt_mm, upto(l, i))
                    if l == 0:
                        dve.wait_ge(tt_init, i + 1)
                    else:
                        dve.wait_ge(tt_copied, upto(l - 1, i))
                    _, right = halves(TT[:], n)
                    if l < LEVELS - 1:
                        _, new = halves(quad(b7), n)
                        nc.vector.tensor_copy(right, new).then_inc(tt_copied, 1)
                    else:
                        nc.vector.tensor_tensor(right, right, part(b7, 0, n), ALU.add).then_inc(tt_copied, 1)

                dve.wait_ge(nxt_done, i + 1)
                dve.wait_ge(r_ready, PRIMED + i)
                nc.vector.tensor_scalar(cur[:, 2], nxt[:, 2], 0.5, None, ALU.mult)
                nc.vector.tensor_scalar(cur[:, 3], nxt[:, 3], 1.0 / DK, None, ALU.mult).then_inc(cur_done, 1)
                level(0)
                x_scale(0)
                add_t(0)
                level(1)
                copy_tt(0)
                x_scale(1)
                level(2)
                add_t(1)
                f_low(j)
                copy_tt(1)
                x_scale(2)
                level(3)
                add_t(2)
                conv(0, j, hn, (1, 2))
                copy_tt(2)
                x_scale(3)
                level(4)
                add_t(3)
                conv(0, j, hn, (3,))
                copy_tt(3)
                x_scale(4)
                level(5)
                add_t(4)
                conv(1, j, hn, (1, 2))
                copy_tt(4)
                x_scale(5)
                level(6)
                add_t(5)
                conv(1, j, hn, (3,))
                copy_tt(5)
                x_scale(6)
                dve.wait_ge(y_mm, i + 1)
                dve.wait_ge(vp_done, i + 1)
                for b in range(B):
                    ins = nc.vector.scalar_tensor_tensor(R[:, b], quad(b4)[:, b], cur[:, 1, b:b + 1], R[:, b], ALU.mult, ALU.add)
                ins.then_inc(r_done, 1)
                copy_tt(6)
                sums(j)
                conv(2, j, hn)
                init_k(j)
                init_t(j)
                dve.wait_ge(o2_done, PRIMED + i + 1)
                dve.wait_ge(gate_done, i + 1)
                nc.vector.scalar_tensor_tensor(G[:], gt[:], 1.0, quad(b6), ALU.add, ALU.mult).then_inc(g_done, 1)
                dve.wait_ge(s_mm, i + 1)
                dve.wait_ge(lvl_upd, upto(6, i))
                dve.wait_ge(blk_done, upto(6, i))
                p128 = PB[:, B * (P - 2):B * (P - 1)]
                for b in range(B):
                    ins = nc.vector.scalar_tensor_tensor(S[:, b], S[:, b], p128[:, b:b + 1], quad(b4)[:, b], ALU.mult, ALU.add)
                ins.then_inc(s_done, 1)
                init_cols(j)
                dve.wait_ge(osum_mm, PRIMED + i + 1)
                dve.wait_ge(cur_done, i + 1)
                nc.vector.tensor_tensor(rr[:, 0], sums_o, cur[:, 3], ALU.mult).then_inc(ms_done, 1)
                dve.wait_ge(ms_done, PRIMED + i + 1)
                nc.vector.tensor_scalar(rr[:, 0], rr[:, 0], EPS_NORM, None, ALU.add).then_inc(ms_eps, 1)
                init_rest(j)
                dve.wait_ge(out_mm, i + 1)
                dve.wait_ge(r_ready, PRIMED + i + 1)
                for b in range(B):
                    bank = (b5, b6)[b // 2]
                    o = acc[:, c, b, :]
                    ins = nc.vector.scalar_tensor_tensor(o, bank[:, (b % 2) * D:(b % 2 + 1) * D], rr[:, 2, b:b + 1], o,
                                                         ALU.mult, ALU.add)
                    if b % 2:
                        ins.then_inc(acc_done, 1)

            dve.wait_ge(s_const, 1)
            over_quads(dve, prologue, body)

            def carry_wait():
                nc.vector.memset(scrap[:], 0.0)

            def stats_of(src, st, ag, ep, g):
                for b in range(B):
                    nc.vector.bn_stats(stats[:, b], src[:, b]).then_inc(st, 1)
                dve.wait_ge(st, B * (g + 1))
                carry_wait()
                for b in range(B):
                    nc.vector.bn_aggr(mv[:, b], stats[:, b]).then_inc(ag, 1)
                dve.wait_ge(ag, B * (g + 1))
                nc.vector.tensor_scalar(rstd[:], mv[:, :, 1], EPS_LN, None, ALU.add).then_inc(ep, 1)

            def normed(src, dst, rs, done, g):
                dve.wait_ge(rs, g + 1)
                for b in range(B):
                    nc.vector.tensor_scalar(dst[:, b], src[:, b], mv[:, b, 0:1], rstd[:, b:b + 1], ALU.subtract, ALU.mult
                                            ).then_inc(done, 1)

            def residual(g):
                dve.wait_ge(m_x, 16 * (g + 1))
                nc.vector.tensor_tensor(x1[:], xn[:], acc[:, g], ALU.add).then_inc(m_y, 1)

            def stats_1(g):
                dve.wait_ge(m_y, g + 1)
                stats_of(x1, m_st, m_ag, m_ep, g)

            def router_logits(g):
                dve.wait_ge(m_lg, g + 1)
                nc.vector.tensor_tensor(logit, lgt, bcast(rbias[:].unsqueeze(1), [P, B, E]), ALU.add).then_inc(m_lb, 1)
                dve.wait_ge(m_lb, g + 1)
                nc.vector.reduce_max(nmax[:], logit, mybir.AxisListType.X).then_inc(m_mx, 1)
                dve.wait_ge(m_mx, g + 1)
                nc.vector.tensor_scalar(nmax[:], nmax[:], -1.0, None, ALU.mult).then_inc(m_nm, 1)

            def router_probs(g):
                dve.wait_ge(m_ex, B * (g + 1))
                nc.vector.reciprocal(den[:, 1], den[:, 0]).then_inc(m_rc, 1)
                dve.wait_ge(m_rc, g + 1)
                nc.vector.tensor_tensor(logit, logit, bcast(den[:, 1].unsqueeze(2), [P, B, E]), ALU.mult).then_inc(m_pr, 1)

            def router_top(g):
                dve.wait_ge(m_pr, g + 1)
                carry_wait()
                for b in range(B):
                    nc.vector.max(top[:, b], logit[:, b]).then_inc(m_tp, 1)
                dve.wait_ge(m_tp, B * (g + 1))
                carry_wait()
                for b in range(B):
                    nc.vector.max_index(topi[:, b], top[:, b], logit[:, b]).then_inc(m_ti, 1)
                nc.vector.tensor_tensor(tsum[:], top[:, :, 0], top[:, :, 1], ALU.add).then_inc(m_ts, 1)
                dve.wait_ge(m_ti, B * (g + 1))
                nc.vector.tensor_copy(topf, topi).then_inc(m_tf, 1)
                dve.wait_ge(m_ts, g + 1)
                nc.vector.tensor_scalar(tsum[:], tsum[:], EPS_TOPK, None, ALU.add).then_inc(m_te, 1)
                dve.wait_ge(m_te, g + 1)
                nc.vector.reciprocal(tsum[:], tsum[:]).then_inc(m_tr2, 1)
                dve.wait_ge(m_tr2, g + 1)
                nc.vector.tensor_tensor(tw[:], top[:, :, 0:2], bcast(tsum[:].unsqueeze(2), [P, B, 2]), ALU.mult).then_inc(m_tw, 1)

            def router_weights(g):
                dve.wait_ge(m_tw, g + 1)
                dve.wait_ge(m_tf, g + 1)
                for x, s in ((0, m_s0), (1, m_s1)):
                    for b in range(B):
                        nc.vector.tensor_scalar(wsel[:, x, b], iot[:], topf[:, b, x:x + 1], tw[:, b, x:x + 1],
                                                ALU.is_equal, ALU.mult).then_inc(s, 1)
                dve.wait_ge(m_s0, B * (g + 1))
                dve.wait_ge(m_s1, B * (g + 1))
                nc.vector.tensor_tensor(wexp[:, 0:E].rearrange("p e b -> p b e"), wsel[:, 0], wsel[:, 1], ALU.add).then_inc(m_we, 1)

            def gate_e(g, e):
                n = g * (E + 1) + e
                dve.wait_ge(silu_e, n + 1)
                wait(dve, dn_mm, PRIMED + n - 1)
                nc.vector.tensor_tensor(hT[e % 2], sg[e % 2], gu[e % 2][1], ALU.mult).then_inc(h_e, 1)

            def sum_expert(g, e):
                n = g * (E + 1) + e
                dve.wait_ge(dn_mm, PRIMED + n + 1)
                if e == 0:
                    dve.wait_ge(m_we, g + 1)
                else:
                    dve.wait_ge(sum_e, PRIMED + n)
                for b in range(B):
                    ins = nc.vector.scalar_tensor_tensor(yo[:, b], dn[e % 2][b // 2][:, b % 2], wexp[:, e, b:b + 1],
                                                         (yo if e else x1)[:, b], ALU.mult, ALU.add)
                ins.then_inc(sum_e, 1)

            def finish(g):
                dve.wait_ge(sum_e, PRIMED + (g + 1) * (E + 1))
                stats_of(yo, m_st2, m_ag2, m_ep2, g)

            def store(g):
                dve.wait_ge(m_out, PRIMED + 16 * g)
                normed(yo, yn, m_rs2, m_yn, g)

            def group(g, first, last):
                router_logits(g)
                if not first:
                    finish(g - 1)
                router_probs(g)
                gate_e(g, 0)
                if not first:
                    store(g - 1)
                router_top(g)
                router_weights(g)
                gate_e(g, 1)
                sum_expert(g, 0)
                for e in range(2, E + 1):
                    gate_e(g, e)
                    sum_expert(g, e - 1)
                    if not last:
                        if e == 8:
                            residual(g + 1)
                        elif e == 9:
                            stats_1(g + 1)
                        elif e == 10:
                            normed(x1, x1, m_rs, m_x1, g + 1)
                sum_expert(g, E)

            dve.wait_ge(acc_done, PRIMED + 2 * H * NCH)
            residual(0)
            stats_1(0)
            normed(x1, x1, m_rs, m_x1, 0)
            group(0, True, False)
            with dve.Fori(1, NCH - 1) as g:
                group(g, False, False)
            group(NCH - 1, False, True)
            finish(NCH - 1)
            store(NCH - 1)

        @block.tensor
        def _(pe):
            def mm(o, l, r, start=True, stop=True, **kw):
                return nc.tensor.matmul(o, l, r, start=start, stop=stop, **kw)

            pe.wait_ge(s_ld, 16 * 13)
            pe.wait_ge(s_const, 1)
            mm(b4[:, 0:H], onesrow, alog)
            for k in range(KT):
                ins = nc.tensor.transpose(b4[:, 64 + k * E:64 + (k + 1) * E], wrn[:, k * P:(k + 1) * P], ident[0:E, 0:E])
            ins.then_inc(s_apm, 1)
            bw = U[:, 0, 0:KT * H].rearrange("p (k h) -> p k h", k=KT)
            with pe.Fori(0, NCH) as c:
                pe.wait_ge(s_xin, 16 * (c + 1))
                pe.wait_ge(s_xcp, PRIMED + c)
                for k in range(KT):
                    for b in range(B):
                        ins = nc.tensor.transpose(pj[:, 0, k, b * P:(b + 1) * P], xnat[:, b, k * P:(k + 1) * P], ident[:])
                ins.then_inc(s_xtr, 1)
                pe.wait_ge(s_xcp, PRIMED + c + 1)
                pe.wait_ge(s_xfc, PRIMED + c)
                for bank, w in ((b5, 0), (b6, 2)):
                    for k in range(KT):
                        ins = mm(bank[:], R[:, w + k], xs[:, k * 512:(k + 1) * 512], start=(k == 0), stop=(k == KT - 1))
                ins.then_inc(s_xfm, 1)
                pe.wait_ge(s_bc, PRIMED + c)
                pe.wait_ge(s_xtc, c + 1)
                for b in range(B):
                    for k in range(KT):
                        ins = mm(b7[:, b * H:(b + 1) * H], xs[:, k * 512 + b * P:k * 512 + (b + 1) * P], bw[:, k],
                                 start=(k == 0), stop=(k == KT - 1))
                ins.then_inc(s_bm, 1)
            pe.wait_ge(s_bc, PRIMED + NCH)
            pe.wait_ge(s_chain["act"], 4)

            def proj(x, j, h, c, pairs=(0, 1)):
                if 0 in pairs:
                    pe.wait_ge(w_loaded[x], 16 * h + 16)
                    if x == 0:
                        wait(pe, conv_done[2], j)
                    elif x == 1:
                        pe.wait_ge(f_relu, j + 1)
                        wait(pe, gate_done, j)
                    elif x == 2:
                        pe.wait_ge(conv_done[0], j + 1)
                for two in pairs:
                    for k in range(KT):
                        ins = mm(pair[x % 2][:, 2 * two:2 * two + 2, 0:W], wqkv[:, x, k], xT[:, k, c, 2 * two:2 * two + 2, :],
                                 start=(k == 0), stop=(k == KT - 1))
                if 1 in pairs:
                    ins.then_inc(proj_done[x], 1)

            def proj_f(j, h, c):
                pe.wait_ge(w_loaded[3], 16 * h + 16)
                wait(pe, ms_done, PRIMED + j - 1)
                mm(bank_f, wf2[:], xf[:, c]).then_inc(proj_done[3], 1)

            def proj_g(j, h, c):
                pe.wait_ge(w_loaded[4], 16 * h + 16)
                pe.wait_ge(conv_done[1], j + 1)
                mm(bank_g, wg2[:], xg[:, c]).then_inc(proj_done[4], 1)

            def sums(x, j):
                src, there = ((sq[:, 0], sq_done[0]), (sq[:, 1], sq_done[1]), (fsp[:, 2], qk_prod))[x]
                pe.wait_ge(conv_done[1], j + 1)
                pe.wait_ge(there, j + 1)
                for b in range(B):
                    ins = mm(sums_qk[:, x, b:b + 1], src[:, b], ones[:])
                if x == 2:
                    ins.then_inc(sums_done, 1)

            def v_turned(j):
                pe.wait_ge(silu_done[2], j + 1)
                for b in range(B):
                    ins = nc.tensor.transpose(quad(b7)[:, b], qkd[:, 2, b], ident[:])
                ins.then_inc(vt_done, 1)

            def prologue(j, h, c):
                proj_f(j, h, c)
                proj(0, j, h, c)
                proj(1, j, h, c)
                proj(2, j, h, c)
                proj_g(j, h, c)
                for x in range(3):
                    sums(x, j)
                v_turned(j)

            def body(i, h, c, hn, cn):
                j = i + 1

                def level(l):
                    n = 1 << l
                    if l == 0:
                        pe.wait_ge(init_done, i + 1)
                        pe.wait_ge(kr_init, i + 1)
                        pe.wait_ge(s_done, PRIMED + i)
                    else:
                        pe.wait_ge(lvl_upd, upto(l - 1, i))
                        pe.wait_ge(qk_done, upto(l - 1, i))
                    right = FQ[:].rearrange("p x b (m two n) -> p x b m two n", two=2, n=n)[:, :, :, :, 1, :]
                    for b in range(B):
                        ins = mm(quad(b4)[:, b], KR[:, b], right[:, :, b])
                    ins.then_inc(lvl_mm, 1)

                def x_(l):
                    n = 1 << l
                    pe.wait_ge(kk_done, upto(l, i))
                    if l == 0:
                        pe.wait_ge(acc_done, PRIMED + 2 * i)
                        for b in range(B):
                            ins = nc.tensor.transpose(quad(b5)[:, b], NT[:, 0, b], ident[:])
                    else:
                        pe.wait_ge(t_add, upto(l - 1, i, LEVELS - 1))
                        left, _ = halves(TM[:], n)
                        for b in range(B):
                            ins = mm(part(b5, 0, n)[:, b], NT[:, l, b], left[:, b])
                    ins.then_inc(x_mm, 1)

                def t_(l):
                    n = 1 << l
                    pe.wait_ge(x_done, upto(l, i))
                    pe.wait_ge(tt_copied, upto(l - 1, i))
                    left, _ = halves(XL[:, l], n)
                    for b in range(B):
                        ins = mm(part(b6, 0, n)[:, b], TT[:, b], left[:, b])
                    ins.then_inc(t_mm, 1)

                def tt_(l):
                    if l == 0:
                        pe.wait_ge(vp_done, i + 1)
                    else:
                        pe.wait_ge(tt_copied, upto(l - 1, i))
                    if l < LEVELS - 1:
                        pe.wait_ge(t_add, upto(l, i, LEVELS - 1))
                        for b in range(B):
                            ins = nc.tensor.transpose(quad(b7)[:, b], TM[:, b], ident[:])
                    else:
                        pe.wait_ge(x_done, upto(l, i))
                        _, right = halves(TT[:], 1 << l)
                        for b in range(B):
                            ins = mm(part(b7, 0, 1 << l)[:, b], XL[:, l, b], right[:, b])
                    ins.then_inc(tt_mm, 1)

                level(0)
                proj_f(j, hn, cn)
                proj(0, j, hn, cn, (0,))
                x_(0)
                level(1)
                tt_(0)
                x_(1)
                level(2)
                t_(1)
                proj(0, j, hn, cn, (1,))
                tt_(1)
                x_(2)
                level(3)
                t_(2)
                proj(1, j, hn, cn, (0,))
                tt_(2)
                x_(3)
                level(4)
                t_(3)
                proj(1, j, hn, cn, (1,))
                tt_(3)
                x_(4)
                level(5)
                t_(4)
                proj(2, j, hn, cn, (0,))
                tt_(4)
                x_(5)
                level(6)
                t_(5)
                proj(2, j, hn, cn, (1,))
                pe.wait_ge(lvl_upd, upto(6, i))
                pe.wait_ge(qk_done, upto(6, i))
                for b in range(B):
                    ins = nc.tensor.transpose(quad(b4)[:, b], KR[:, b], ident[:])
                ins.then_inc(krt_mm, 1)
                tt_(5)
                x_(6)
                sums(0, j)
                proj_g(j, hn, cn)
                pe.wait_ge(krt_done, i + 1)
                for b in range(B):
                    ins = mm(quad(b4)[:, b], FQ[:, 0, b], S[:, b])
                ins.then_inc(y_mm, 1)
                sums(1, j)
                tt_(6)
                sums(2, j)
                pe.wait_ge(tt_copied, upto(6, i))
                pe.wait_ge(r_done, i + 1)
                for b in range(B):
                    ins = mm(quad(b5)[:, b], TT[:, b], R[:, b])
                ins.then_inc(u_mm, 1)
                for b in range(B):
                    mm(quad(b6)[:, b], S[:, b], FQ[:, 1, b], start=(b == 0), stop=False, skip_group_check=True)
                pe.wait_ge(u_done, i + 1)
                for b in range(B):
                    ins = mm(quad(b6)[:, b], U[:, b], AT[:, b], start=False, stop=(b == B - 1), skip_group_check=True)
                ins.then_inc(o_mm, 1)
                for b in range(B):
                    ins = mm(quad(b4)[:, b], KRt[:, b], U[:, b])
                ins.then_inc(s_mm, 1)
                v_turned(j)
                pe.wait_ge(o2_done, PRIMED + i + 1)
                pe.wait_ge(sums_read, j + 1)
                for b in range(B):
                    ins = mm(sums_o[:, b:b + 1], sq[:, 0, b], ones[:])
                ins.then_inc(osum_mm, 1)
                pe.wait_ge(g_done, i + 1)
                for b in range(B):
                    ins = mm((b5, b6)[b // 2][:, (b % 2) * D:(b % 2 + 1) * D], G[:, b], ow[:, h, :])
                ins.then_inc(out_mm, 1)

            over_quads(pe, prologue, body)

            def turn_x1(g):
                pe.wait_ge(m_x1, B * (g + 1))
                for k in range(KT):
                    for b in range(B):
                        ins = nc.tensor.transpose(x1t[:, k, b * P:(b + 1) * P], x1[:, b, k * P:(k + 1) * P], ident[:])
                ins.then_inc(m_tr, 1)

            def gate_up(g, e):
                n = g * (E + 1) + e
                if e == 1:
                    pe.wait_ge(m_lb, g + 1)
                wait(pe, h_e, PRIMED + n - 1)
                for x in range(2):
                    for k in range(KT):
                        ins = mm(pj[:, e % 2, x], wgu[:, k, e, x * I:(x + 1) * I], x1T[:, k], start=(k == 0), stop=(k == KT - 1))
                ins.then_inc(gu_mm, 1)

            def down(g, e):
                n = g * (E + 1) + e
                pe.wait_ge(h_e, PRIMED + n + 1)
                wait(pe, sum_e, PRIMED + n - 1)
                for b in range(B):
                    ins = mm(dn[e % 2][b // 2][:, b % 2], hT[e % 2][:, b], wdn[:, e, :])
                ins.then_inc(dn_mm, 1)

            def group(g, last):
                pe.wait_ge(m_xT, g + 1)
                for b in range(B):
                    for k in range(KT):
                        ins = mm(lgt[:, b], x1T[:, k, b * P:(b + 1) * P], wrT[:, k], start=(k == 0), stop=(k == KT - 1))
                ins.then_inc(m_lg, 1)
                gate_up(g, 0)
                for e in range(E - 1):
                    gate_up(g, e + 1)
                    down(g, e)
                gate_up(g, E)
                if not last:
                    pe.wait_ge(h_e, PRIMED + g * (E + 1) + E)
                    turn_x1(g + 1)
                down(g, E - 1)
                down(g, E)

            pe.wait_ge(gate_done, H * NCH + 1)
            turn_x1(0)
            pe.wait_ge(m_w, 16 * 10)
            with pe.Fori(0, NCH - 1) as g:
                group(g, False)
            group(NCH - 1, True)


NAMES = {"x": "L0_attn_hidden_states"}
NAMES.update({n: "L0_attn_" + n for n in (
    "q_w", "k_w", "v_w", "q_conv_w", "k_conv_w", "v_conv_w", "f_w1", "f_w2", "b_w", "A_log", "dt_bias",
    "g_w1", "g_w2", "g_b2", "o_norm_w", "o_w")})
NAMES.update({n: "L0_ffn_" + n for n in ("Wr", "bias", "Wg", "Wu", "Wd", "sWg", "sWu", "sWd")})


def kernel(**inputs):
    import concourse.bacc as bacc
    from concourse.bass_utils import run_bass_kernel_spmd

    nc = bacc.Bacc("TRN2", target_bir_lowering=False, num_devices=1)
    arrays, aps = {}, {}
    for short, name in NAMES.items():
        v = np.ascontiguousarray(inputs[name])
        arrays[f"in_{name}"] = v
        aps[short] = nc.dram_tensor(f"in_{name}", v.shape, mybir.dt.from_np(v.dtype), kind="ExternalInput").ap()
    out = nc.dram_tensor("out", (B, T, D), FP, kind="ExternalOutput").ap()
    build(nc, aps, out)
    r = run_bass_kernel_spmd(nc, [arrays], core_ids=[0])
    return r.results[0]["out"]
```
